# Optimizing a Trainium2 kernel written in Bass

```python
import numpy as np
import jax
import jax.numpy as jnp

def _softmax(x, axis=-1):
    return jax.nn.softmax(x, axis=axis)

def _gelu(x):
    return jax.nn.gelu(x, approximate=True)

def _silu(x):
    return jax.nn.silu(x)

def _sigmoid(x):
    return jax.nn.sigmoid(x)

def _layernorm(x, axis=-1, eps=1e-05):
    m = jnp.mean(x, axis=axis, keepdims=True)
    v = jnp.var(x, axis=axis, keepdims=True)
    return (x - m) / jnp.sqrt(v + eps)

def _scatter_add(tgt, idx, src, axis=0):
    return tgt.at[idx].add(src)

def _segment_sum(src, seg, n):
    return jax.ops.segment_sum(src, seg, n)
kernel_name = 'mk_prb_d1_jaxref_r4_b363d1'

def setup_inputs(seed: int=0):
    np.random.seed(seed)
    _w = jnp.asarray

    def _L0_attn_setup():
        import jax, jax.numpy as jnp
        import numpy as np
        BSZ, L, D, N = (2, 512, 256, 16)
        key = jax.random.key(seed)
        ks = jax.random.split(key, 6)
        x = jax.random.normal(ks[0], (BSZ, L, D), dtype=jnp.float32)
        A = -0.5 - 0.5 * jax.random.uniform(ks[1], (D, N), dtype=jnp.float32)
        s = 1.0 / np.sqrt(D)
        W_delta = jax.random.normal(ks[2], (D, D), dtype=jnp.float32) * s
        delta_bias = jnp.zeros((D,), dtype=jnp.float32)
        W_B = jax.random.normal(ks[3], (D * N, D), dtype=jnp.float32) * s
        W_C = jax.random.normal(ks[4], (D * N, D), dtype=jnp.float32) * s
        return {'x': x, 'A': A, 'W_delta': W_delta, 'delta_bias': delta_bias, 'W_B': W_B, 'W_C': W_C}
    _L0_attn_in = _L0_attn_setup()

    def _L0_ffn_setup():
        import jax, jax.numpy as jnp
        import numpy as np
        E = 8
        K = 2
        D = 256
        P = 1024
        key = jax.random.key(seed)
        ks = jax.random.split(key, 8)
        s = lambda fan_in: 1.0 / np.sqrt(fan_in)
        x = jax.random.normal(ks[0], (2, 512, D), dtype=jnp.float32)
        W1 = jax.random.normal(ks[1], (E, D, P), dtype=jnp.float32) * s(D)
        b1 = jax.random.normal(ks[2], (E, P), dtype=jnp.float32) * 0.01
        W2 = jax.random.normal(ks[3], (E, P, D), dtype=jnp.float32) * s(P)
        b2 = jax.random.normal(ks[4], (E, D), dtype=jnp.float32) * 0.01
        Wr = jax.random.normal(ks[5], (D, E), dtype=jnp.float32) * s(D)
        br = jax.random.normal(ks[6], (E,), dtype=jnp.float32) * 0.01
        return {'x': x, 'W1': W1, 'b1': b1, 'W2': W2, 'b2': b2, 'Wr': Wr, 'br': br}
    _L0_ffn_in = _L0_ffn_setup()
    _d = {'L0_attn_x': _L0_attn_in['x'], 'L0_attn_A': _L0_attn_in['A'], 'L0_attn_W_delta': _L0_attn_in['W_delta'], 'L0_attn_delta_bias': _L0_attn_in['delta_bias'], 'L0_attn_W_B': _L0_attn_in['W_B'], 'L0_attn_W_C': _L0_attn_in['W_C'], 'L0_ffn_W1': _L0_ffn_in['W1'], 'L0_ffn_b1': _L0_ffn_in['b1'], 'L0_ffn_W2': _L0_ffn_in['W2'], 'L0_ffn_b2': _L0_ffn_in['b2'], 'L0_ffn_Wr': _L0_ffn_in['Wr'], 'L0_ffn_br': _L0_ffn_in['br']}
    _x0 = _d['L0_attn_x']
    _d['L0_attn_x'] = jax.random.normal(jax.random.fold_in(jax.random.key(seed), 1), (2, 2048, 256), dtype=_x0.dtype)
    del _x0
    return _d

def reference(L0_attn_x, L0_attn_A, L0_attn_W_delta, L0_attn_delta_bias, L0_attn_W_B, L0_attn_W_C, L0_ffn_W1, L0_ffn_b1, L0_ffn_W2, L0_ffn_b2, L0_ffn_Wr, L0_ffn_br):

    def _L0_attn_ref(x, A, W_delta, delta_bias, W_B, W_C):
        import jax, jax.numpy as jnp
        import numpy as np
        BSZ, L, D, N = (2, 512, 256, 16)
        B_, L_, D_ = x.shape
        N_ = A.shape[1]
        delta = jax.nn.softplus(jnp.einsum('bld,ed->ble', x, W_delta) + delta_bias)
        B_sel = jnp.einsum('bld,ed->ble', x, W_B).reshape(B_, L_, D_, N_)
        C_sel = jnp.einsum('bld,ed->ble', x, W_C).reshape(B_, L_, D_, N_)

        def step(h, inp):
            x_t, delta_t, B_t, C_t = inp
            dA = delta_t[..., None] * A
            A_bar = jnp.exp(dA)
            B_bar = (A_bar - 1.0) / A * B_t
            h = A_bar * h + B_bar * x_t[..., None]
            y_t = jnp.sum(h * C_t, axis=-1)
            return (h, y_t)
        h0 = jnp.zeros((B_, D_, N_), dtype=x.dtype)
        seq = (jnp.moveaxis(x, 1, 0), jnp.moveaxis(delta, 1, 0), jnp.moveaxis(B_sel, 1, 0), jnp.moveaxis(C_sel, 1, 0))
        _, ys = jax.lax.scan(step, h0, seq)
        return jnp.moveaxis(ys, 0, 1)

    def _L0_ffn_ref(x, W1, b1, W2, b2, Wr, br):
        import jax, jax.numpy as jnp
        import numpy as np
        E = 8
        K = 2
        D = 256
        P = 1024
        B, S, _ = x.shape
        xf = x.reshape(B * S, D)
        scores = xf @ Wr + br
        _, top_idx = jax.lax.top_k(scores, K)
        mask = jax.nn.one_hot(top_idx, E, dtype=scores.dtype).sum(-2) > 0
        router_weights = jax.nn.softmax(jnp.where(mask, scores, -jnp.inf), axis=-1)
        h = jax.nn.gelu(jnp.einsum('td,edp->etp', xf, W1) + b1[:, None, :])
        y = jnp.einsum('etp,epd->etd', h, W2) + b2[:, None, :]
        out = jnp.einsum('te,etd->td', router_weights, y)
        return out.reshape(B, S, D)
    x = L0_attn_x
    xn = _layernorm(x, axis=-1)
    x = x + _L0_attn_ref(xn, L0_attn_A, L0_attn_W_delta, L0_attn_delta_bias, L0_attn_W_B, L0_attn_W_C) + _L0_ffn_ref(xn, L0_ffn_W1, L0_ffn_b1, L0_ffn_W2, L0_ffn_b2, L0_ffn_Wr, L0_ffn_br)
    return x

_drawn_inputs = setup_inputs


def setup_inputs(seed=0):
    import zlib

    import numpy as np

    out = dict(_drawn_inputs(seed))
    spreads = {'L0_attn_delta_bias': (0.0, 0.1)}
    factors = {'L0_ffn_b1': 38.052, 'L0_ffn_b2': 25.632, 'L0_ffn_br': 5.714}
    for name, (base, spread) in spreads.items():
        noise = np.random.default_rng([zlib.crc32(name.encode()), seed]).standard_normal(out[name].shape)
        drawn = base * np.exp(spread * noise) if base else spread * noise
        out[name] = jnp.asarray(drawn.astype(out[name].dtype))
    for name, factor in factors.items():
        out[name] = (out[name] * factor).astype(out[name].dtype)
    return out
```

```python
from contextlib import ExitStack

import concourse.bass as bass
import concourse.mybir as mybir
from concourse.alu_op_type import AluOpType as ALU

F32 = mybir.dt.float32
F16 = mybir.dt.float16
I32 = mybir.dt.int32
U32 = mybir.dt.uint32
ACT = mybir.ActivationFunctionType
AX = mybir.AxisListType

P = 128
B, L, D = 2, 2048, 256
T = B * L
N = 16
E = 8
F = 1024
KC = D // P
FC = F // P
NT = T // P
CH = 512
CT = CH // P
NCH = T // CH
RCH = L // CH
EPS = 1e-5
WSCALE = 64.0
BT = 256
BS = BT // P
NBLK = 2 * T // BT + E - 1
NSLOT = NBLK * BT
MAXB = T // BT
BIG = 3.0e38
TILES = KC * N
PIECE = 1024
NPIECE = 4


class Chain:

    def __init__(self, eng, sem):
        self.eng, self.sem, self.n = eng, sem, 0

    def run(self, ins):
        self.n += 1
        ins.then_inc(self.sem, 1)
        self.eng.wait_ge(self.sem, self.n)


def project_z(nc, keep, out, c, done):
    for hf in range(KC):
        k = 0
        for kc in range(KC):
            for a, b in ((0, 0), (0, 1), (1, 0)):
                k += 1
                ins = nc.tensor.matmul(out[hf][:], keep["Wd"][:, a, kc, hf * P:(hf + 1) * P],
                                       keep["xT"][:, bass.ds(c, 1), b, kc, :].squeeze(1),
                                       start=(k == 1), stop=(k == 3 * KC))
    ins.then_inc(done, 1)


def softplus_parts(nc, act, keep, src, z_ready, z_count, chain, chain_at, taken, ln_done):
    act.wait_ge(z_ready, z_count)
    for hf in range(KC):
        bias = keep["dbias"][:, hf:hf + 1]
        nc.scalar.activation(keep["zt"][:, hf], src[hf][:], ACT.Abs, scale=1.0 / WSCALE, bias=bias).then_inc(chain, 1)
        ins = nc.scalar.activation(keep["rel"][:, hf], src[hf][:], ACT.Relu, scale=1.0 / WSCALE, bias=bias)
        if taken is not None:
            ins.then_inc(taken, 1)
    act.wait_ge(chain, chain_at + KC)
    nc.scalar.activation(keep["zt"][:], keep["zt"][:], ACT.Exp, scale=-1.0).then_inc(chain, 1)
    act.wait_ge(chain, chain_at + (KC + 1))
    nc.scalar.activation(keep["zt"][:], keep["zt"][:], ACT.Ln, bias=1.0).then_inc(ln_done, 1)


def prologue(nc, io, keep, banks, ctx):
    def sb(name, shape, dt):
        return ctx.enter_context(nc.sbuf_tensor(name, shape, dt))

    def sem(name):
        return ctx.enter_context(nc.semaphore(name))

    GN = 2
    GW = GN * D
    NG = N // GN
    stB, stC = (keep["yall"][:, m:m + 2].rearrange("p a b c -> p (a b c)").rearrange(
        "p (r c m) -> p r c m", r=2, c=KC) for m in (0, 2))
    xall = keep["xall"]
    xcur = sb("xcur", [P, 2, CT, D], F32)
    stWd = sb("stWd", [P, KC, D], F32)
    Wd = keep["Wd"]
    stWr = sb("stWr", [P, KC, E], F32)
    Wr = sb("Wr", [P, 2, KC, E], F16)
    brb = sb("brb", [P, E], F32)
    stats = sb("stats", [P, NT, 6], F32)
    mean = sb("mean", [P, NT], F32)
    rstd = sb("rstd", [P, NT], F32)
    va = sb("va", [P, NT], F32)
    vb = sb("vb", [P, NT], F32)
    ident = keep["ident"]
    ones = sb("ones", [P, P], F16)
    tri = sb("tri", [P, P], F16)
    rev = sb("rev", [P, E], F32)
    thr = sb("thr", [P, MAXB], F32)
    blk = sb("blk", [P, NBLK], F32)
    one_r = sb("one_r", [P, NT * E], F32)
    wscale = sb("wscale", [P, 1], F32)
    zero = keep["yall"][:, NCH - 1, 0, 0:D]
    rel, zt, dcur = keep["rel"], keep["zt"], keep["dcur"]

    small_in = sem("small_in")
    wgrp_in = [sem("wgrp_in0"), sem("wgrp_in1")]
    XP = 4
    x_in = [sem(f"x_in{k}") for k in range(XP)]
    consts = sem("consts")
    zero_set = sem("zero_set")
    b_hi = sem("b_hi")
    b_lo = sem("b_lo")
    c_hi = sem("c_hi")
    c_lo = sem("c_lo")
    wd_hi = sem("wd_hi")
    wd_lo = sem("wd_lo")
    stat_chain = sem("stat_chain")
    act_chain = sem("act_chain")
    var_ready = sem("var_ready")
    std_ready = sem("std_ready")
    xn_ready = sem("xn_ready")
    xn_kept = sem("xn_kept")
    c_scaled = sem("c_scaled")
    xt_ready = sem("xt_ready")
    xt_hi = sem("xt_hi")
    xt_lo = sem("xt_lo")
    gap_ready = sem("gap_ready")
    gap_exp = sem("gap_exp")
    cnt_ready = sem("cnt_ready")
    cnt_sum = sem("cnt_sum")
    sc_ready = sem("sc_ready")
    z_ready = sem("z_ready")
    z_chain = sem("z_chain")
    ln_ready = sem("ln_ready")
    delta_ready = sem("delta_ready")

    wb_v = io["WBT"].rearrange("(c p) m -> p c m", p=P)
    wc_v = io["WCT"].rearrange("(c p) m -> p c m", p=P)
    WB = keep["WB"][:].rearrange("p h c n d -> p h c (n d)")
    WC = keep["WC"][:].rearrange("p h c n d -> p h c (n d)")
    xT = keep["xT"]

    def router_sb(name):
        return sb(name, [P, NT, E], F32)

    sc, oh1, oh2, tmp = router_sb("sc"), router_sb("oh1"), router_sb("oh2"), router_sb("tmp")
    mx = sb("mx", [P, 2, NT], F32)
    top = sb("top", [P, NT], F32)
    M = sb("M", [P, E, NT], F32)
    cs = sb("cs", [P, E, NT], F32)
    rowc = sb("rowc", [P, E], F16)
    before = sb("before", [P, E], F32)
    nblk = sb("nblk", [P, E], F32)
    endb = sb("endb", [P, E], F32)
    off = sb("off", [P, E], F32)
    cmpb = sb("cmpb", [P, E, MAXB], F32)
    cmpe = sb("cmpe", [P, NBLK, E], F32)
    slotf = sb("slotf", [P, 2, NT], F32)
    ebf = sb("ebf", [P, NBLK], F32)

    def xt_at(part, kc, i, par, lo=0, n=CH):
        return xT[:, bass.ds(i * 2 + par, 1), part, kc, lo:lo + n].squeeze(1)

    block = ctx.enter_context(nc.Block())

    @block.sync
    def _(sp):
        for k in range(XP):
            tiles = slice(k * NT // XP, (k + 1) * NT // XP)
            sp.dma_start(xall[:, tiles, :], io["x_tok"][:, tiles, :]).then_inc(x_in[k], 16)
        sp.dma_start(stWd[:], io["WdT"].rearrange("(c p) m -> p c m", p=P)).then_inc(small_in, 16)
        sp.dma_start(stWr[:], io["Wr"].rearrange("(c p) m -> p c m", p=P)).then_inc(small_in, 16)
        sp.dma_start(brb[:], io["br"].partition_broadcast(P)).then_inc(small_in, 16)
        sp.dma_start(keep["A"][:], io["A"].rearrange("(h p) n -> p h n", p=P)).then_inc(small_in, 16)
        sp.dma_start(keep["dbias"][:], io["dbias"]).then_inc(small_in, 16)
        with sp.Fori(0, NG // 2) as i:
            for par in range(2):
                sp.wait_ge(b_lo, i * 2 + (par + 1))
                sp.wait_ge(c_lo, i * 2 + (par + 1))
                at = i * (2 * GW) + par * GW
                sp.dma_start(stB[:, par], wb_v[:, :, bass.ds(at, GW)]).then_inc(wgrp_in[par], 16)
                sp.dma_start(stC[:, par], wc_v[:, :, bass.ds(at, GW)]).then_inc(wgrp_in[par], 16)
        sp.wait_ge(zero_set, 1)
        sp.dma_start(io["xs"].rearrange("(p r) d -> p r d", p=P),
                     zero.unsqueeze(1).broadcast_to([P, NSLOT // P, D])).then_inc(keep["zeros_out"], 16)

    @block.gpsimd
    def _(pool):
        pool.sem_inc(c_lo, 2)
        nc.gpsimd.memset(zero, 0.0).then_inc(zero_set, 1)
        nc.gpsimd.memset(ident[:], 0.0)
        nc.gpsimd.memset(tri[:], 1.0)
        nc.gpsimd.memset(ones[:], 1.0)
        nc.gpsimd.memset(wscale[:], WSCALE)
        nc.gpsimd.memset(one_r[:], 1.0).then_inc(consts, 1)
        pool.wait_ge(consts, 1)
        nc.gpsimd.affine_select(out=ident[:], in_=ident[:], compare_op=ALU.not_equal, fill=1.0, base=0,
                                pattern=[[-1, P]], channel_multiplier=1)
        nc.gpsimd.affine_select(out=tri[:], in_=tri[:], compare_op=ALU.is_gt, fill=0.0, base=0,
                                pattern=[[1, P]], channel_multiplier=-1)
        nc.gpsimd.iota(rev[:], pattern=[[-1, E]], base=E, channel_multiplier=0,
                       allow_small_or_imprecise_dtypes=True)
        nc.gpsimd.iota(thr[:], pattern=[[BT, MAXB]], base=0, channel_multiplier=0,
                       allow_small_or_imprecise_dtypes=True)
        nc.gpsimd.iota(blk[:], pattern=[[1, NBLK]], base=0, channel_multiplier=0,
                       allow_small_or_imprecise_dtypes=True).then_inc(consts, 1)
        with pool.Fori(0, NG // 2) as i:
            for par in range(2):
                pool.wait_ge(c_hi, i * 2 + (par + 1))
                nc.gpsimd.tensor_tensor(stC[:, par], stC[:, par],
                                        wscale[:].unsqueeze(2).broadcast_to(list(stC[:, par].shape)),
                                        ALU.mult).then_inc(c_scaled, 1)
                pool.wait_ge(c_scaled, i * 2 + (par + 1))
                at = i * (2 * GW) + par * GW
                nc.gpsimd.tensor_tensor(WC[:, 1, :, bass.ds(at, GW)], stC[:, par], WC[:, 0, :, bass.ds(at, GW)],
                                        ALU.subtract).then_inc(c_lo, 1)
        pool.wait_ge(ln_ready, 1)
        nc.gpsimd.tensor_tensor(dcur[:, 0], rel[:, 0], zt[:, 0], ALU.add).then_inc(delta_ready, 1)
        pool.wait_ge(delta_ready, 1)

    @block.scalar
    def _(act):
        act.wait_ge(small_in, 80)
        nc.scalar.activation(stWd[:], stWd[:], ACT.Copy, scale=WSCALE).then_inc(act_chain, 1)
        nc.scalar.activation(stWr[:], stWr[:], ACT.Copy, scale=WSCALE).then_inc(act_chain, 1)
        act.wait_ge(act_chain, 2)
        nc.scalar.activation(Wd[:, 0], stWd[:], ACT.Copy).then_inc(wd_hi, 1)
        nc.scalar.activation(Wr[:, 0], stWr[:], ACT.Copy).then_inc(wd_hi, 1)
        act.wait_ge(var_ready, 1)
        nc.scalar.activation(va[:], vb[:], ACT.Sqrt).then_inc(std_ready, 1)

        def weight_group(i, par):
            at = i * (2 * GW) + par * GW
            act.wait_ge(wgrp_in[par], i * 32 + 32)
            nc.scalar.activation(WB[:, 0, :, bass.ds(at, GW)], stB[:, par], ACT.Copy, scale=WSCALE).then_inc(b_hi, 1)
            nc.scalar.activation(WC[:, 0, :, bass.ds(at, GW)], stC[:, par], ACT.Copy, scale=WSCALE).then_inc(c_hi, 1)

        with act.Fori(0, NCH // 2) as i:
            for par in range(2):
                weight_group(i, par)
                for kc in range(KC):
                    act.wait_ge(xt_ready, i * (2 * KC) + ((par + 2) * KC + kc + 1))
                    nc.scalar.activation(xt_at(0, kc, i, par), banks[par * KC + kc][:], ACT.Copy).then_inc(xt_hi, 1)
        softplus_parts(nc, act, keep, banks[4:6], z_ready, 1, z_chain, 0, None, ln_ready)
        act.wait_ge(gap_ready, 1)
        nc.scalar.activation(keep["w"][:, 1, :], keep["w"][:, 0, :], ACT.Exp).then_inc(gap_exp, 1)

    @block.vector
    def _(dve):
        v = nc.vector
        dve.sem_inc(xn_kept, 2)
        dve.sem_inc(b_lo, 2)
        dve.sem_inc(xt_lo, 2 * KC)
        for k in range(XP):
            dve.wait_ge(x_in[k], 16)
            with dve.Fori(k * NT // XP // 4, (k + 1) * NT // XP // 4) as i:
                for q in range(4):
                    one = bass.ds(i * 4 + q, 1)
                    v.bn_stats(stats[:, one, :].rearrange("p a b -> p (a b)"),
                               xall[:, one, :].rearrange("p a b -> p (a b)")).then_inc(stat_chain, 1)
        ch = Chain(dve, stat_chain)
        ch.n = NT
        dve.wait_ge(stat_chain, ch.n)
        m_e, q_e, m_o, q_o = stats[:, :, 1], stats[:, :, 2], stats[:, :, 4], stats[:, :, 5]
        ch.run(v.tensor_tensor(mean[:], m_e, m_o, ALU.add))
        ch.run(v.tensor_scalar(mean[:], mean[:], 0.5, None, ALU.mult))
        ch.run(v.tensor_tensor(va[:], m_e, m_o, ALU.subtract))
        ch.run(v.scalar_tensor_tensor(va[:], va[:], 0.25, va[:], ALU.mult, ALU.mult))
        ch.run(v.tensor_tensor(vb[:], q_e, q_o, ALU.add))
        ch.run(v.scalar_tensor_tensor(vb[:], vb[:], 1.0 / D, va[:], ALU.mult, ALU.add))
        ch.run(v.tensor_scalar(vb[:], vb[:], EPS, None, ALU.add))
        dve.sem_inc(var_ready, 1)
        dve.wait_ge(std_ready, 1)
        ch.run(v.reciprocal(rstd[:], va[:]))
        ch.run(v.tensor_tensor(va[:], rstd[:], rstd[:], ALU.mult))
        ch.run(v.tensor_tensor(va[:], va[:], vb[:], ALU.mult))
        ch.run(v.tensor_scalar(va[:], va[:], -0.5, 1.5, ALU.mult, ALU.add))
        ch.run(v.tensor_tensor(rstd[:], rstd[:], va[:], ALU.mult))
        dve.wait_ge(wd_hi, 2)
        v.reciprocal(keep["rA"][:], keep["A"][:])
        v.tensor_tensor(Wd[:, 1], stWd[:], Wd[:, 0], ALU.subtract).then_inc(wd_lo, 1)
        v.tensor_tensor(Wr[:, 1], stWr[:], Wr[:, 0], ALU.subtract).then_inc(wd_lo, 1)
        with dve.Fori(0, NCH // 2) as i:
            for par in range(2):
                dve.wait_ge(xn_kept, i * 2 + (par + 1))
                dve.wait_ge(xt_ready, i * (2 * KC) + KC * (par + 1))
                for q in range(CT):
                    t = i * (2 * CT) + (par * CT + q)
                    ins = v.tensor_scalar(xcur[:, par, q, :], xall[:, bass.ds(t, 1), :].rearrange("p a b -> p (a b)"),
                                          mean[:, bass.ds(t, 1)], rstd[:, bass.ds(t, 1)],
                                          ALU.subtract, ALU.mult)
                ins.then_inc(xn_ready, 1)
                dve.wait_ge(xn_ready, i * 2 + (par + 1))
                v.tensor_scalar(xall[:, bass.ds(i * (2 * CT) + par * CT, CT), :], xcur[:, par], 1.0, None,
                                ALU.mult).then_inc(xn_kept, 1)
            for par in range(2):
                at = i * (2 * GW) + par * GW
                dve.wait_ge(b_hi, i * 2 + (par + 1))
                v.scalar_tensor_tensor(WB[:, 1, :, bass.ds(at, GW)], stB[:, par], WSCALE, WB[:, 0, :, bass.ds(at, GW)],
                                       ALU.mult, ALU.subtract).then_inc(b_lo, 1)
                for kc in range(KC):
                    dve.wait_ge(xt_hi, i * (2 * KC) + (par * KC + kc + 1))
                    v.tensor_tensor(xt_at(1, kc, i, par), banks[par * KC + kc][:], xt_at(0, kc, i, par),
                                    ALU.subtract).then_inc(xt_lo, 1)

        dve.wait_ge(sc_ready, NCH)
        dve.wait_ge(consts, 2)

        def per_token(ap):
            return ap.unsqueeze(2).broadcast_to([P, NT, E])

        def per_expert(ap):
            return ap.unsqueeze(1).broadcast_to([P, NT, E])

        sc_ps = banks[6][:, 0:NT * E].rearrange("p (i e) -> p i e", e=E)
        ch.run(v.scalar_tensor_tensor(sc[:], sc_ps, 1.0 / WSCALE, per_expert(brb[:]), ALU.mult, ALU.add))
        for k, oh in ((0, oh1), (1, oh2)):
            ch.run(v.tensor_reduce(mx[:, k, :], sc[:], AX.X, ALU.max))
            ch.run(v.tensor_tensor(tmp[:], sc[:], per_token(mx[:, k, :]), ALU.is_equal))
            ch.run(v.tensor_tensor(tmp[:], tmp[:], per_expert(rev[:]), ALU.mult))
            ch.run(v.tensor_reduce(top[:], tmp[:], AX.X, ALU.max))
            ch.run(v.tensor_tensor(oh[:], per_expert(rev[:]), per_token(top[:]), ALU.is_equal))
            if k == 0:
                ch.run(v.scalar_tensor_tensor(sc[:], oh[:], -BIG, sc[:], ALU.mult, ALU.add))
        ch.run(v.tensor_tensor(keep["w"][:, 0, :], mx[:, 1, :], mx[:, 0, :], ALU.subtract))
        dve.sem_inc(gap_ready, 1)
        ch.run(v.tensor_tensor(M[:].rearrange("p e i -> p i e"), oh1[:], oh2[:], ALU.add))
        ch.run(v.tensor_tensor_scan(cs[:].rearrange("p e i -> p (e i)"), one_r[:], M[:].rearrange("p e i -> p (e i)"),
                                    0.0, ALU.mult, ALU.add))
        last = cs[:, :, NT - 1]
        ch.run(v.memset(before[:, 0:1], 0.0))
        ch.run(v.tensor_copy(before[:, 1:E], cs[:, 0:E - 1, NT - 1]))
        ch.run(v.tensor_tensor(rowc[:], last, before[:], ALU.subtract))
        dve.sem_inc(cnt_ready, 1)
        ch.run(v.tensor_tensor(cs[:], cs[:], M[:], ALU.subtract))
        dve.wait_ge(cnt_sum, 1)
        earlier, total = banks[7][:, 0:E], banks[7][:, E:2 * E]
        ch.run(v.tensor_tensor(cmpb[:], total.unsqueeze(2).broadcast_to([P, E, MAXB]),
                               thr[:].unsqueeze(1).broadcast_to([P, E, MAXB]), ALU.is_gt))
        ch.run(v.tensor_reduce(nblk[:], cmpb[:], AX.X, ALU.add))
        ch.run(v.tensor_tensor_scan(endb[:], one_r[:, 0:E], nblk[:], 0.0, ALU.mult, ALU.add))
        ch.run(v.tensor_tensor(off[:], endb[:], nblk[:], ALU.subtract))
        ch.run(v.scalar_tensor_tensor(off[:], off[:], float(BT), earlier, ALU.mult, ALU.add))
        ch.run(v.tensor_tensor(off[:], off[:], before[:], ALU.subtract))
        ch.run(v.tensor_tensor(cs[:], cs[:], off[:].unsqueeze(2).broadcast_to([P, E, NT]), ALU.add))
        for k, oh in ((0, oh1), (1, oh2)):
            ch.run(v.tensor_tensor(tmp[:], oh[:], cs[:].rearrange("p e i -> p i e"), ALU.mult))
            ch.run(v.tensor_reduce(slotf[:, k, :], tmp[:], AX.X, ALU.add))
        ch.run(v.tensor_copy(keep["slot"][:], slotf[:]))
        ch.run(v.tensor_tensor(cmpe[:], endb[:].unsqueeze(1).broadcast_to([P, NBLK, E]),
                               blk[:].unsqueeze(2).broadcast_to([P, NBLK, E]), ALU.is_le))
        ch.run(v.tensor_reduce(ebf[:], cmpe[:], AX.X, ALU.add))
        ch.run(v.tensor_scalar(keep["eblk"][:], ebf[:], float(E - 1), None, ALU.min))
        dve.wait_ge(gap_exp, 1)
        ch.run(v.tensor_scalar(top[:], keep["w"][:, 1, :], 1.0, None, ALU.add))
        ch.run(v.reciprocal(keep["w"][:, 0, :], top[:]))
        ch.run(v.tensor_tensor(keep["w"][:, 1, :], keep["w"][:, 1, :], keep["w"][:, 0, :], ALU.mult))

    @block.tensor
    def _(pe):
        mm = nc.tensor.matmul
        pe.sem_inc(xt_ready, 2 * KC)
        pe.wait_ge(consts, 2)
        pe.wait_ge(wd_lo, 2)
        with pe.Fori(0, NCH // 2) as i:
            for par in range(2):
                pe.wait_ge(xn_ready, i * 2 + par + 1)
                pe.wait_ge(xt_lo, i * (2 * KC) + KC * (par + 1))
                for kc in range(KC):
                    for q in range(CT):
                        ins = nc.tensor.transpose(banks[par * KC + kc][:, q * P:(q + 1) * P],
                                                  xcur[:, par, q, kc * P:(kc + 1) * P], ident[:])
                    ins.then_inc(xt_ready, 1)
            for par in range(2):
                at = i * (2 * CH) + par * CH
                pe.wait_ge(xt_lo, i * (2 * KC) + (par + 3) * KC)
                for q in range(CT):
                    n = 0
                    for kc in range(KC):
                        for a, b in ((0, 0), (0, 1), (1, 0), (1, 1)):
                            n += 1
                            ins = mm(banks[6][:, bass.ds(i * (2 * CT * E) + (par * CT + q) * E, E)],
                                     xt_at(a, kc, i, par, q * P, P), Wr[:, b, kc, :],
                                     start=(n == 1), stop=(n == 4 * KC))
                ins.then_inc(sc_ready, 1)
        project_z(nc, keep, banks[4:6], 0, z_ready)
        pe.wait_ge(cnt_ready, 1)
        mm(banks[7][:, 0:E], tri[:], rowc[:], start=True, stop=True)
        mm(banks[7][:, E:2 * E], ones[:], rowc[:], start=True, stop=True).then_inc(cnt_sum, 1)


def scan_phase(nc, io, keep, banks, ctx, row):
    split_weights, combine = row == 0, row == 1

    def sb(name, shape, dt):
        return ctx.enter_context(nc.sbuf_tensor(f"{name}_{row}", shape, dt))

    def sem(name):
        return ctx.enter_context(nc.semaphore(f"{name}_{row}"))

    AR = 4
    aexp = sb("aexp", [P, AR, CH], F32)
    ub = sb("ub", [P, 2, CH], F32)
    uxb = sb("uxb", [P, 2, CH], F32)
    hb = sb("hb", [P, AR, CH], F32)
    hcb = sb("hcb", [P, 2, CH], F32)
    x32 = sb("x32", [P, KC, CH], F32)
    state = sb("state", [P, TILES], F32)
    Bps, Cps, Yps, Ops = banks[0:2], banks[2:4], banks[4:6], banks[6:8]
    xT, WB, WC, A = keep["xT"], keep["WB"], keep["WC"], keep["A"]
    rel, zt, dcur, yall = keep["rel"], keep["zt"], keep["dcur"], keep["yall"]

    a_ready = sem("a_ready")
    B_ready = sem("B_ready")
    C_ready = sem("C_ready")
    u_done = sem("u_done")
    ux_done = sem("ux_done")
    h_done = sem("h_done")
    hc_done = sem("hc_done")
    acc_done = sem("acc_done")
    state_saved = sem("state_saved")
    x32_done = sem("x32_done")
    z_ready = sem("z_ready")
    z_taken = sem("z_taken")
    z_chain = sem("z_chain")
    ln_done = sem("ln_done")
    delta_done = sem("delta_done")
    U_CR, UX_CR, H_CR, HC_CR, ACC_CR, ST_CR, D_CR = 2, 1, AR, 2, 1, AR, 1
    ACCS = TILES - KC
    Z_AT, Z_LOG, D_NEXT, D_HERE = 3, 6, 20, 2

    if split_weights:
        stage = yall[:, RCH:NCH].rearrange("p a b c -> p (a b c)")
        wst = stage[:, 0:2 * PIECE].rearrange("p (r f) -> p r f", r=2)
        whl = stage[:, 2 * PIECE:4 * PIECE].bitcast(F16).rearrange("p (r h f) -> p r h f", r=2, h=2)
        piece_in = [sem("piece_in0"), sem("piece_in1")]
        piece_out = [sem("piece_out0"), sem("piece_out1")]
        p_scaled = sem("p_scaled")
        p_hi = sem("p_hi")
        p_lo = sem("p_lo")
    if combine:
        gat = xT[:, 0:RCH].rearrange("p a b c d -> p (a b c d)").bitcast(F32).rearrange(
            "p (g q k d) -> p g q k d", g=2, q=CT, k=2)
        ycur = sb("ycur", [P, 2, KC, CH], F32)
        xres = sb("xres", [P, 2, CT, D], F32)
        ob = sb("ob", [P, 2, CT, D], F32)
        sidx = sb("sidx", [P, 2, 2, CT], U32)
        ycur_done = sem("ycur_done")
        idx_done = sem("idx_done")
        turned = sem("turned")
        gathered = [sem("gathered0"), sem("gathered1")]
        xres_in = [sem("xres_in0"), sem("xres_in1")]
        o_ready = sem("o_ready")
        closing_ready = sem("closing_ready")
        o_step = sem("o_step")
        out_sent = [sem("out_sent0"), sem("out_sent1")]
    STEPS = 2 * CT

    def tile(s):
        return s // N, s % N

    def chunk(t, c):
        return t[:, bass.ds(c + row * RCH, 1)].squeeze(1)

    def group_chunk(c, g, last):
        return NCH - 1 if last and g == 0 else c + 3 * g

    def group_at(c, g, last):
        return c * 2 + (1 - g if last else g)

    def group_tiles(c, g, last):
        return bass.ds(group_chunk(c, g, last) * CT, CT)

    def chunks(eng, body):
        if combine:
            with eng.Fori(0, RCH - 1) as c:
                body(c, False)
            body(RCH - 1, True)
        else:
            with eng.Fori(0, RCH) as c:
                body(c, False)

    def add_x(eng, ops, c, g, last, done):
        eng.wait_ge(xres_in[g], c * 16 + 16)
        eng.wait_ge(o_step, group_at(c, g, last) * STEPS + 2 * STEPS)
        ops.tensor_tensor(ob[:, g], ob[:, g], xres[:, g], ALU.add).then_inc(done, 1)

    PIECES = E * NPIECE // RCH
    EPC = E // RCH
    STRIDE = 3

    def store_piece(sp, c, k):
        ex = c * EPC + k // NPIECE
        sp.wait_ge(p_lo, c * PIECES + (k + 1 + 2))
        sp.dma_start(io["wsplit"][bass.ds(ex, 1), :, k % NPIECE, :, :].rearrange("a p h f -> p (a h) f"),
                     whl[:, k % 2]).then_inc(piece_out[k % 2], 16)

    block = ctx.enter_context(nc.Block())

    @block.sync
    def _(sp):
        if split_weights:
            with sp.Fori(0, RCH) as c:
                for k in range(PIECES):
                    par = k % 2
                    ex = c * EPC + k // NPIECE
                    pc = k % NPIECE
                    sp.wait_ge(p_lo, c * PIECES + (k + 1))
                    if pc < KC:
                        src = io["W1"][bass.ds(ex, 1), pc * P:(pc + 1) * P, :].rearrange("a p f -> p (a f)")
                        sp.dma_start(wst[:, par, :], src).then_inc(piece_in[par], 16)
                    else:
                        fc = (pc - KC) * (FC // 2)
                        src = io["W2"][bass.ds(ex, 1), fc * P:(fc + FC // 2) * P, :]\
                            .rearrange("a (c p) d -> p (a c) d", p=P)
                        sp.dma_start(wst[:, par, :].rearrange("p (c d) -> p c d", d=D), src).then_inc(piece_in[par], 16)
                    if k >= 1:
                        store_piece(sp, c, k - 1)
                store_piece(sp, c, PIECES - 1)
            for par in range(2):
                sp.wait_ge(piece_out[par], (RCH * PIECES // 2 + 1) * 16)

        def body(c, last):
            order = (1, 0) if last else (0, 1)
            for g in order:
                sp.wait_ge(o_ready, c * 2 + (g + 1))
                sp.dma_start(xres[:, g], io["x_tok"][:, group_tiles(c, g, last), :]).then_inc(xres_in[g], 16)
            for g in order:
                if last and g == 0:
                    sp.wait_ge(closing_ready, 1)
                else:
                    sp.wait_ge(o_ready, group_at(c, g, last) + 3)
                sp.dma_start(io["out_tok"][:, group_tiles(c, g, last), :], ob[:, g]).then_inc(out_sent[g], 16)

        if combine:
            chunks(sp, body)
            for g in range(2):
                sp.wait_ge(out_sent[g], (RCH + 1) * 16)

    @block.scalar
    def _(act):
        act.sem_inc(state_saved, ST_CR)
        if split_weights:
            act.wait_ge(keep["zeros_out"], 16)
        act.sem_inc(z_taken, KC)

        def save_state(c, s):
            act.wait_ge(h_done, c * TILES + (s + 1 + H_CR))
            nc.scalar.activation(state[:, s:s + 1], hb[:, s % AR, CH - 1:CH], ACT.Copy).then_inc(state_saved, 1)

        def body(c, last):
            for s in range(TILES):
                hf, n = tile(s)
                if n == 0:
                    act.wait_ge(delta_done, c * 2 + (hf + 1))
                act.wait_ge(h_done, c * TILES + (s + 1))
                nc.scalar.activation(aexp[:, s % AR], dcur[:, hf, :], ACT.Exp,
                                     scale=A[:, hf, n:n + 1]).then_inc(a_ready, 1)
                if s >= 3:
                    save_state(c, s - 3)
                if s == Z_LOG and not last:
                    act.wait_ge(delta_done, c * 2 + 2)
                    softplus_parts(nc, act, keep, Ops, z_ready, c + 1, z_chain, c * (KC + 1), z_taken, ln_done)
                if split_weights and s % STRIDE == 1 and s // STRIDE < PIECES:
                    k = s // STRIDE
                    par = k % 2
                    act.wait_ge(piece_in[par], (c * (PIECES // 2) + (k // 2 + 1)) * 16)
                    nc.scalar.activation(wst[:, par, :], wst[:, par, :], ACT.Copy, scale=WSCALE).then_inc(p_scaled, 1)
                    act.wait_ge(piece_out[par], (c * (PIECES // 2) + (k // 2 + 1)) * 16)
                    act.wait_ge(p_scaled, c * PIECES + (k + 1))
                    nc.scalar.activation(whl[:, par, 0, :], wst[:, par, :], ACT.Copy).then_inc(p_hi, 1)
                if combine and s in (5, 19) and not (last and s == 5):
                    take_y(c, s // 19, last)
            for s in range(TILES - 3, TILES):
                save_state(c, s)
            if last:
                take_y(c, 0, last)

        def take_y(c, g, last):
            act.wait_ge(acc_done, (c + (1 if last and g == 0 else 0)) * ACCS + 1)
            act.wait_ge(turned, group_at(c, g, last) + 1)
            nc.scalar.activation(ycur[:, g], yall[:, bass.ds(group_chunk(c, g, last), 1)].squeeze(1), ACT.Copy,
                                 scale=1.0 / (WSCALE * WSCALE)).then_inc(ycur_done, 1)

        chunks(act, body)

    @block.gpsimd
    def _(pool):
        pool.sem_inc(ux_done, UX_CR)
        pool.sem_inc(delta_done, D_CR)
        if split_weights:
            pool.sem_inc(p_lo, 2)
            pool.sem_inc(piece_out[0], 16)
            pool.sem_inc(piece_out[1], 16)
            pool.wait_ge(keep["zeros_out"], 16)
        if combine:
            pool.sem_inc(out_sent[0], 16)
            pool.sem_inc(out_sent[1], 16)
            pool.sem_inc(o_ready, 2)

        def body(c, last, scatter=()):
            pool.wait_ge(ux_done, c * TILES + 1)
            nc.gpsimd.tensor_tensor(x32[:], chunk(xT, c)[:, 0], chunk(xT, c)[:, 1], ALU.add).then_inc(x32_done, 1)
            pool.wait_ge(x32_done, c + 1)
            if combine:
                pool.wait_ge(o_ready, c * 2 + 2)
                for g in range(2):
                    ins = nc.gpsimd.tensor_copy(sidx[:, g], keep["slot"][:, :, group_tiles(c, g, last)])
                ins.then_inc(idx_done, 1)
                pool.wait_ge(idx_done, c + 1)
            for s in range(TILES):
                hf, n = tile(s)
                pool.wait_ge(u_done, c * TILES + (s + 1 + U_CR))
                pool.wait_ge(h_done, c * TILES + (s + AR - 1))
                nc.gpsimd.tensor_tensor(uxb[:, s % 2], ub[:, s % 2], x32[:, hf], ALU.mult).then_inc(ux_done, 1)
                if s == D_HERE:
                    pool.wait_ge(a_ready, c * TILES + 1)
                    nc.gpsimd.tensor_tensor(dcur[:, 1], rel[:, 1], zt[:, 1], ALU.add).then_inc(delta_done, 1)
                if s == D_NEXT and not last:
                    pool.wait_ge(a_ready, c * TILES + N)
                    pool.wait_ge(ln_done, c + 1)
                    nc.gpsimd.tensor_tensor(dcur[:, 0], rel[:, 0], zt[:, 0], ALU.add).then_inc(delta_done, 1)
                if split_weights and s % STRIDE == 2 and s // STRIDE < PIECES:
                    k = s // STRIDE
                    par = k % 2
                    pool.wait_ge(p_hi, c * PIECES + (k + 1))
                    nc.gpsimd.tensor_tensor(whl[:, par, 1, :], wst[:, par, :], whl[:, par, 0, :],
                                            ALU.subtract).then_inc(p_lo, 1)
                for i, k in scatter[s // 2:s // 2 + 1] if s % 2 == 0 else ():
                    nc.gpsimd.indirect_dma_start(
                        out=io["xs"], out_offset=bass.IndirectOffsetOnAxis(keep["slot"][:, k, i:i + 1], 0),
                        in_=keep["xall"][:, i, :], in_offset=None).then_inc(keep["scattered"], 16)
                if combine and s == 19 and not last:
                    add_x(pool, nc.gpsimd, c, 0, last, o_ready)
                if combine and s == 31:
                    add_x(pool, nc.gpsimd, c, 1, last, o_ready)
                if combine and s < 4 * CT:
                    g, q, k = s // (2 * CT), s % (2 * CT) // 2, s % 2
                    nc.gpsimd.indirect_dma_start(
                        out=gat[:, g, q, k, :], out_offset=None, in_=io["ys"],
                        in_offset=bass.IndirectOffsetOnAxis(sidx[:, g, k, q:q + 1], 0)).then_inc(gathered[g], 16)

        if split_weights:
            todo = [(i, k) for i in range(NT) for k in range(2)]
            for c in range(RCH):
                body(c, False, todo[c * len(todo) // RCH:(c + 1) * len(todo) // RCH])
            pool.wait_ge(keep["scattered"], len(todo) * 16)
        else:
            chunks(pool, body)

    @block.vector
    def _(dve):
        v = nc.vector
        dve.sem_inc(u_done, U_CR)
        dve.sem_inc(h_done, H_CR)
        dve.sem_inc(hc_done, HC_CR)
        dve.sem_inc(acc_done, ACC_CR)
        if combine:
            dve.sem_inc(o_step, STEPS)
        v.memset(state[:], 0.0)

        def u_op(c, s):
            dve.wait_ge(a_ready, c * TILES + (s + 1))
            dve.wait_ge(B_ready, c * TILES + (s + 1))
            v.scalar_tensor_tensor(ub[:, s % 2], aexp[:, s % AR], -1.0, Bps[s % 2][:], ALU.add,
                                   ALU.mult).then_inc(u_done, 1)

        def scan_op(c, s):
            dve.wait_ge(ux_done, c * TILES + (s + 1 + UX_CR))
            dve.wait_ge(state_saved, c * TILES + (s + 1))
            v.tensor_tensor_scan(hb[:, s % AR], aexp[:, s % AR], uxb[:, s % 2], state[:, s:s + 1],
                                 ALU.mult, ALU.add).then_inc(h_done, 1)

        def hc_op(c, s):
            hf, n = tile(s)
            dve.wait_ge(C_ready, c * TILES + (s + 1))
            dve.wait_ge(h_done, c * TILES + (s + 1 + H_CR))
            dst = Yps[hf][:] if n == 0 else hcb[:, s % 2]
            v.scalar_tensor_tensor(dst, hb[:, s % AR], keep["rA"][:, hf, n:n + 1], Cps[s % 2][:], ALU.mult,
                                   ALU.mult).then_inc(hc_done, 1)

        def acc_op(c, s):
            hf, n = tile(s)
            if n == 0:
                return
            dve.wait_ge(hc_done, c * TILES + (s + 1 + HC_CR))
            dve.wait_ge(acc_done, c * ACCS + (hf * (N - 1) + n - 1 + ACC_CR))
            dst = chunk(yall, c)[:, hf] if n == N - 1 else Yps[hf][:]
            v.tensor_tensor(dst, Yps[hf][:], hcb[:, s % 2], ALU.add).then_inc(acc_done, 1)

        def out_op(c, g, k, last):
            q = k % CT
            at = group_at(c, g, last)
            tok = bass.ds(group_chunk(c, g, last) * CT + q, 1)
            if k < CT:
                if k == 0:
                    dve.wait_ge(gathered[g], c * (2 * CT * 16) + 2 * CT * 16)
                    dve.wait_ge(out_sent[g], c * 16 + 16)
                    dve.wait_ge(turned, at + 3)
                v.scalar_tensor_tensor(ob[:, g, q], gat[:, g, q, 0], keep["w"][:, 0, tok],
                                       Ops[q // 2][:, q % 2 * D:(q % 2 + 1) * D], ALU.mult, ALU.add).then_inc(o_step, 1)
            elif k < STEPS:
                dve.wait_ge(o_step, at * STEPS + (q + 1 + STEPS))
                v.scalar_tensor_tensor(ob[:, g, q], gat[:, g, q, 1], keep["w"][:, 1, tok], ob[:, g, q],
                                       ALU.mult, ALU.add).then_inc(o_step, 1)
            else:
                add_x(dve, v, c, g, last, closing_ready)

        def body(c, last):
            for s in range(TILES):
                u_op(c, s)
                if s >= 1:
                    scan_op(c, s - 1)
                if s >= 2:
                    acc_op(c, s - 2)
                if s >= 1:
                    hc_op(c, s - 1)
                if combine and not last and 10 <= s < 10 + STEPS:
                    out_op(c, 0, s - 10, last)
                if combine and 22 <= s < 22 + STEPS:
                    out_op(c, 1, s - 22, last)
            scan_op(c, TILES - 1)
            acc_op(c, TILES - 2)
            hc_op(c, TILES - 1)
            acc_op(c, TILES - 1)
            if last:
                for k in range(STEPS + 1):
                    out_op(c, 0, k, last)

        chunks(dve, body)

    @block.tensor
    def _(pe):
        mm = nc.tensor.matmul
        if combine:
            pe.sem_inc(turned, 2)

        def project(bank, W, c, s, done):
            hf, n = tile(s)
            k = 0
            for kc in range(KC):
                for a, b in ((0, 0), (0, 1), (1, 0)):
                    k += 1
                    ins = mm(bank[:], W[:, a, kc, n, hf * P:(hf + 1) * P], chunk(xT, c)[:, b, kc, :],
                             start=(k == 1), stop=(k == 3 * KC))
            ins.then_inc(done, 1)

        def project_c(c, s):
            pe.wait_ge(hc_done, c * TILES + (s + 1))
            project(Cps[s % 2], WC, c, s, C_ready)

        def turn(c, g, last):
            pe.wait_ge(ycur_done, group_at(c, g, last) + 1)
            pe.wait_ge(o_step, group_at(c, g, last) * STEPS + CT)
            pe.wait_ge(z_taken, (c + (0 if last else 1)) * KC + KC)
            for q in range(CT):
                for hf in range(KC):
                    col = q % 2 * D + hf * P
                    ins = nc.tensor.transpose(Ops[q // 2][:, col:col + P], ycur[:, g, hf, q * P:(q + 1) * P],
                                              keep["ident"][:])
            ins.then_inc(turned, 1)

        def body(c, last):
            for s in range(TILES):
                pe.wait_ge(u_done, c * TILES + (s + 1))
                project(Bps[s % 2], WB, c, s, B_ready)
                if s >= 1:
                    project_c(c, s - 1)
                if s == Z_AT and not last:
                    if combine:
                        pe.wait_ge(o_step, c * (2 * STEPS) + CT)
                    pe.wait_ge(z_taken, c * KC + KC)
                    project_z(nc, keep, Ops, c + (row * RCH + 1), z_ready)
                if combine and s == 8 and not last:
                    turn(c, 0, last)
                if combine and s == 21:
                    turn(c, 1, last)
            project_c(c, TILES - 1)
            if last:
                turn(c, 0, last)

        chunks(pe, body)


def expert_phase(nc, io, keep, banks, ctx):
    def sb(name, shape, dt):
        return ctx.enter_context(nc.sbuf_tensor(name, shape, dt))

    def sem(name):
        return ctx.enter_context(nc.semaphore(name))

    w1 = keep["xT"][:, 0:RCH].rearrange("p a b c d -> p (a b c d)").rearrange(
        "p (r c h f) -> p r c h f", r=2, c=KC, h=2)
    hs = sb("hs", [P, 2, 2, FC, BT], F16)
    w2 = sb("w2", [P, 2, 2, 2, FC // 2, D], F16)
    b1 = sb("b1", [P, 2, FC], F32)
    b2 = sb("b2", [P, 2, D], F32)
    xb = sb("xb", [P, 2, BS, D], F32)
    xbt = sb("xbt", [P, 2, 2, KC, BT], F16)
    h32 = sb("h32", [P, FC, BT], F32)
    yo = sb("yo", [P, 2, BS, D], F32)
    Hps, Tps, Yps = banks[0:4], banks[4:6], banks[6:8]

    w1_in = [sem("w1_in0"), sem("w1_in1")]
    w2_in = [sem("w2_in0"), sem("w2_in1")]
    xb_in = [sem("xb_in0"), sem("xb_in1")]
    y_out = [sem("y_out0"), sem("y_out1")]
    T_done = sem("T_done")
    H_done = sem("H_done")
    Y_done = sem("Y_done")
    xhi_done = sem("xhi_done")
    xlo_done = sem("xlo_done")
    gelu_done = sem("gelu_done")
    hhi_done = sem("hhi_done")
    hlo_done = sem("hlo_done")
    y_taken = sem("y_taken")
    PAIRS = FC // 2
    xs_v = io["xs"].rearrange("(b s p) d -> p b s d", s=BS, p=P)
    ys_v = io["ys"].rearrange("(b s p) d -> p b s d", s=BS, p=P)

    block = ctx.enter_context(nc.Block())


    @block.sync
    def _(sp):
        def load_slots(b, par):
            sp.wait_ge(T_done, b + 1)
            sp.dma_start(xb[:, par], xs_v[:, bass.ds(b, 1)].rearrange("p b s d -> p (b s) d")).then_inc(xb_in[par], 16)

        def load_w1(b, par):
            ex = sp.value_load(keep["eblk"][0:1, bass.ds(b, 1)], min_val=0, max_val=E - 1)
            sp.wait_ge(H_done, b * PAIRS + PAIRS)
            sp.wait_ge(gelu_done, b * FC + FC)
            sp.dma_start(w1[:, par], io["wsplit"][bass.ds(ex, 1), :, 0:KC].rearrange("a p c h f -> p (a c) h f"))\
                .then_inc(w1_in[par], 16)
            sp.dma_start(b1[:, par], io["b1"][bass.ds(ex, 1)].rearrange("a p c -> p (a c)")).then_inc(w1_in[par], 16)

        def store(b, par):
            sp.wait_ge(y_taken, b + (1 + 2))
            sp.dma_start(ys_v[:, bass.ds(b, 1)].rearrange("p b s d -> p (b s) d"), yo[:, par]).then_inc(y_out[par], 16)

        sp.sem_inc(y_out[0], 16)
        sp.sem_inc(y_out[1], 16)
        sp.wait_ge(keep["scattered"], 2 * NT * 16)
        load_slots(0, 0)
        load_w1(0, 0)
        load_slots(1, 1)
        load_w1(1, 1)
        load_slots(2, 0)
        load_w1(2, 0)
        load_slots(3, 1)
        with sp.Fori(0, (NBLK - 5) // 2) as i:
            for m in range(2):
                load_w1(i * 2 + (m + 3), (m + 1) % 2)
                load_slots(i * 2 + (m + 4), m)
                store(i * 2 + m, m)
        load_w1(NBLK - 2, 1)
        load_slots(NBLK - 1, 0)
        store(NBLK - 5, 0)
        load_w1(NBLK - 1, 0)
        for b in range(NBLK - 4, NBLK):
            store(b, b % 2)
        sp.wait_ge(y_out[0], (NBLK // 2 + 2) * 16)
        sp.wait_ge(y_out[1], (NBLK // 2 + 1) * 16)

    @block.gpsimd
    def _(pool):
        def load(b, par):
            ex = pool.value_load(keep["eblk"][0:1, bass.ds(b, 1)], min_val=0, max_val=E - 1)
            pool.wait_ge(y_taken, b + 1)
            pool.dma_start(w2[:, par].rearrange("p c h f d -> p c h (f d)"),
                           io["wsplit"][bass.ds(ex, 1), :, KC:NPIECE].rearrange("a p c h f -> p (a c) h f"))\
                .then_inc(w2_in[par], 16)
            pool.dma_start(b2[:, par], io["b2"][bass.ds(ex, 1), :].broadcast_to([P, D])).then_inc(w2_in[par], 16)

        pool.wait_ge(w1_in[0], 32)
        with pool.Fori(0, NBLK // 2) as i:
            for par in range(2):
                load(i * 2 + par, par)
        load(NBLK - 1, 0)

    @block.tensor
    def _(pe):
        mm = nc.tensor.matmul
        pe.sem_inc(T_done, 2)
        pe.sem_inc(H_done, 2 * PAIRS)
        pe.sem_inc(Y_done, 2)

        def turn(b, par, half):
            pe.wait_ge(xb_in[par], half * 16 + 16)
            pe.wait_ge(xlo_done, b + 1)
            for kc in range(KC):
                for s in range(BS):
                    ins = nc.tensor.transpose(Tps[par][:, kc * BT + s * P:kc * BT + (s + 1) * P],
                                              xb[:, par, s, kc * P:(kc + 1) * P], keep["ident"][:])
            ins.then_inc(T_done, 1)

        def hidden(b, par, half):
            pe.wait_ge(xlo_done, b + 1 + 2)
            pe.wait_ge(w1_in[par], half * 32 + 32)
            for fc in range(FC):
                if fc % 2 == 0:
                    pe.wait_ge(gelu_done, b * FC + (FC + fc + 2))
                k = 0
                for kc in range(KC):
                    for a, c in ((0, 0), (0, 1), (1, 0)):
                        k += 1
                        ins = mm(Hps[fc // 2][:, fc % 2 * BT:(fc % 2 + 1) * BT], w1[:, par, kc, a, fc * P:(fc + 1) * P],
                                 xbt[:, par, c, kc, :], start=(k == 1), stop=(k == 3 * KC))
                if fc % 2 == 1:
                    ins.then_inc(H_done, 1)

        def down(b, par, half):
            pe.wait_ge(w2_in[par], half * 32 + 32)
            pe.wait_ge(y_taken, b + 1)
            pe.wait_ge(hlo_done, b * 2 + 2 + 4)
            for s in range(BS):
                k = 0
                for fc in range(FC):
                    for a, c in ((0, 0), (0, 1), (1, 0)):
                        k += 1
                        ins = mm(Yps[par][:, s * D:(s + 1) * D], hs[:, par, a, fc, s * P:(s + 1) * P],
                                 w2[:, par, fc // (FC // 2), c, fc % (FC // 2), :],
                                 start=(k == 1), stop=(k == 3 * FC))
            ins.then_inc(Y_done, 1)

        turn(0, 0, 0)
        hidden(0, 0, 0)
        turn(1, 1, 0)
        with pe.Fori(0, NBLK // 2 - 1) as i:
            hidden(i * 2 + 1, 1, i)
            turn(i * 2 + 2, 0, i + 1)
            down(i * 2, 0, i)
            hidden(i * 2 + 2, 0, i + 1)
            turn(i * 2 + 3, 1, i + 1)
            down(i * 2 + 1, 1, i)
        hidden(NBLK - 2, 1, NBLK // 2 - 1)
        turn(NBLK - 1, 0, NBLK // 2)
        down(NBLK - 3, 0, NBLK // 2 - 1)
        hidden(NBLK - 1, 0, NBLK // 2)
        down(NBLK - 2, 1, NBLK // 2 - 1)
        down(NBLK - 1, 0, NBLK // 2)

    @block.scalar
    def _(act):
        act.sem_inc(gelu_done, 2 * FC)

        def x_high(b, par):
            act.wait_ge(T_done, b + 1 + 2)
            act.wait_ge(H_done, b * PAIRS + PAIRS)
            nc.scalar.activation(xbt[:, par, 0].rearrange("p c s -> p (c s)"), Tps[par][:], ACT.Copy).then_inc(xhi_done, 1)

        def gelus(b, par, half):
            act.wait_ge(w1_in[par], half * 32 + 32)
            for fc in range(FC):
                if fc % 2 == 0:
                    act.wait_ge(H_done, b * PAIRS + (fc // 2 + 1 + 2 * PAIRS))
                if fc % (FC // 2) == 0:
                    act.wait_ge(hlo_done, b * 2 + (fc // (FC // 2) + 1 + 2))
                nc.scalar.activation(h32[:, fc, :], Hps[fc // 2][:, fc % 2 * BT:(fc % 2 + 1) * BT],
                                     ACT.Gelu_apprx_tanh, bias=b1[:, par, fc:fc + 1],
                                     scale=1.0 / WSCALE).then_inc(gelu_done, 1)

        x_high(0, 0)
        with act.Fori(0, NBLK // 2) as i:
            gelus(i * 2, 0, i)
            x_high(i * 2 + 1, 1)
            gelus(i * 2 + 1, 1, i)
            x_high(i * 2 + 2, 0)
        gelus(NBLK - 1, 0, NBLK // 2)

    @block.vector
    def _(dve):
        v = nc.vector
        dve.sem_inc(xlo_done, 2)
        dve.sem_inc(hlo_done, 4)
        dve.sem_inc(y_taken, 2)

        def x_low(b, par):
            dve.wait_ge(xhi_done, b + 1)
            v.tensor_tensor(xbt[:, par, 1].rearrange("p c s -> p (c s)"), Tps[par][:],
                            xbt[:, par, 0].rearrange("p c s -> p (c s)"), ALU.subtract).then_inc(xlo_done, 1)

        def split_h(b, par):
            dve.wait_ge(Y_done, b + 1)
            for q in range(2):
                fs = slice(q * (FC // 2), (q + 1) * (FC // 2))
                dve.wait_ge(gelu_done, b * FC + ((q + 1) * (FC // 2) + 2 * FC))
                v.tensor_copy(hs[:, par, 0, fs, :], h32[:, fs, :]).then_inc(hhi_done, 1)
                dve.wait_ge(hhi_done, b * 2 + (q + 1))
                v.tensor_tensor(hs[:, par, 1, fs, :], h32[:, fs, :], hs[:, par, 0, fs, :],
                                ALU.subtract).then_inc(hlo_done, 1)

        def take_y(b, par, half):
            dve.wait_ge(Y_done, b + 1 + 2)
            dve.wait_ge(y_out[par], half * 16 + 16)
            v.scalar_tensor_tensor(yo[:, par], Yps[par][:].rearrange("p (s d) -> p s d", d=D), 1.0 / WSCALE,
                                   b2[:, par].unsqueeze(1).broadcast_to([P, BS, D]), ALU.mult,
                                   ALU.add).then_inc(y_taken, 1)

        x_low(0, 0)
        split_h(0, 0)
        x_low(1, 1)
        with dve.Fori(0, NBLK // 2 - 1) as i:
            split_h(i * 2 + 1, 1)
            x_low(i * 2 + 2, 0)
            take_y(i * 2, 0, i)
            split_h(i * 2 + 2, 0)
            x_low(i * 2 + 3, 1)
            take_y(i * 2 + 1, 1, i)
        split_h(NBLK - 2, 1)
        x_low(NBLK - 1, 0)
        take_y(NBLK - 3, 0, NBLK // 2 - 1)
        split_h(NBLK - 1, 0)
        take_y(NBLK - 2, 1, NBLK // 2 - 1)
        take_y(NBLK - 1, 0, NBLK // 2)


def program(nc, io):
    io["xs"] = nc.dram_tensor("xs", [NSLOT, D], F32).ap()
    io["ys"] = nc.dram_tensor("ys", [NSLOT, D], F32).ap()
    io["wsplit"] = nc.dram_tensor("wsplit", [E, P, NPIECE, 2, PIECE], F16).ap()
    io["x_tok"] = io["x"].rearrange("b (i p) d -> p (b i) d", p=P)
    io["out_tok"] = io["out"].rearrange("b (i p) d -> p (b i) d", p=P)
    with ExitStack() as ctx:
        keep = {}

        def kp(name, shape, dt):
            keep[name] = ctx.enter_context(nc.sbuf_tensor(f"k_{name}", shape, dt))

        kp("WB", [P, 2, KC, N, D], F16)
        kp("WC", [P, 2, KC, N, D], F16)
        kp("xT", [P, NCH, 2, KC, CH], F16)
        kp("Wd", [P, 2, KC, D], F16)
        kp("rel", [P, KC, CH], F32)
        kp("zt", [P, KC, CH], F32)
        kp("dcur", [P, KC, CH], F32)
        kp("yall", [P, NCH, KC, CH], F32)
        kp("A", [P, KC, N], F32)
        kp("rA", [P, KC, N], F32)
        kp("dbias", [P, KC], F32)
        kp("ident", [P, P], F32)
        kp("w", [P, 2, NT], F32)
        kp("slot", [P, 2, NT], U32)
        kp("eblk", [P, NBLK], I32)
        keep["scattered"] = ctx.enter_context(nc.semaphore("scattered"))
        keep["zeros_out"] = ctx.enter_context(nc.semaphore("zeros_out"))
        banks = [ctx.enter_context(nc.psum_tensor(f"bank{i}", [P, 512], F32)) for i in range(8)]
        with ExitStack() as rows:
            keep["xall"] = rows.enter_context(nc.sbuf_tensor("xall", [P, NT, D], F32))
            with ExitStack() as c1:
                prologue(nc, io, keep, banks, c1)
            with ExitStack() as c1:
                scan_phase(nc, io, keep, banks, c1, 0)
        with ExitStack() as c1:
            expert_phase(nc, io, keep, banks, c1)
        with ExitStack() as c1:
            scan_phase(nc, io, keep, banks, c1, 1)


def kernel(**inputs):
    import numpy as np
    import concourse.bacc as bacc
    from concourse.bass_utils import run_bass_kernel_spmd

    a = {k: np.asarray(v) for k, v in inputs.items()}
    arrays = {
        "x": a["L0_attn_x"],
        "A": a["L0_attn_A"],
        "WdT": a["L0_attn_W_delta"].T,
        "dbias": a["L0_attn_delta_bias"].reshape(KC, P).T,
        "WBT": a["L0_attn_W_B"].reshape(D, N, D).transpose(2, 1, 0).reshape(D, N * D),
        "WCT": a["L0_attn_W_C"].reshape(D, N, D).transpose(2, 1, 0).reshape(D, N * D),
        "W1": a["L0_ffn_W1"],
        "b1": a["L0_ffn_b1"].reshape(E, FC, P).transpose(0, 2, 1),
        "W2": a["L0_ffn_W2"],
        "b2": a["L0_ffn_b2"],
        "Wr": a["L0_ffn_Wr"],
        "br": a["L0_ffn_br"],
    }
    arrays = {k: np.ascontiguousarray(v) for k, v in arrays.items()}
    nc = bacc.Bacc("TRN2", target_bir_lowering=False, num_devices=1)
    io = {k: nc.dram_tensor(f"in_{k}", v.shape, mybir.dt.from_np(v.dtype), kind="ExternalInput").ap()
          for k, v in arrays.items()}
    io["out"] = nc.dram_tensor("out", (B, L, D), F32, kind="ExternalOutput").ap()
    program(nc, io)
    r = run_bass_kernel_spmd(nc, [{f"in_{k}": v for k, v in arrays.items()}], core_ids=[0])
    return r.results[0]["out"]
```

```python
from contextlib import ExitStack

import concourse.bass as bass
import concourse.mybir as mybir
from concourse.alu_op_type import AluOpType as ALU

F32 = mybir.dt.float32
F16 = mybir.dt.float16
I32 = mybir.dt.int32
U32 = mybir.dt.uint32
ACT = mybir.ActivationFunctionType
AX = mybir.AxisListType

P = 128
B, L, D = 2, 2048, 256
T = B * L
N = 16
E = 8
F = 1024
KC = D // P
FC = F // P
NT = T // P
CH = 512
CT = CH // P
NCH = T // CH
RCH = L // CH
EPS = 1e-5
WSCALE = 64.0
BT = 256
BS = BT // P
NBLK = 2 * T // BT + E - 1
NSLOT = NBLK * BT
MAXB = T // BT
BIG = 3.0e38
TILES = KC * N
PIECE = 1024
NPIECE = 4


class Chain:

    def __init__(self, eng, sem):
        self.eng, self.sem, self.n = eng, sem, 0

    def run(self, ins):
        self.n += 1
        ins.then_inc(self.sem, 1)
        self.eng.wait_ge(self.sem, self.n)


def project_z(nc, keep, out, c, done):
    for hf in range(KC):
        k = 0
        for kc in range(KC):
            for a, b in ((0, 0), (0, 1), (1, 0)):
                k += 1
                ins = nc.tensor.matmul(out[hf][:], keep["Wd"][:, a, kc, hf * P:(hf + 1) * P],
                                       keep["xT"][:, bass.ds(c, 1), b, kc, :].squeeze(1),
                                       start=(k == 1), stop=(k == 3 * KC))
    ins.then_inc(done, 1)


def softplus_parts(nc, act, keep, src, z_ready, z_count, chain, chain_at, taken, ln_done):
    act.wait_ge(z_ready, z_count)
    for hf in range(KC):
        bias = keep["dbias"][:, hf:hf + 1]
        nc.scalar.activation(keep["zt"][:, hf], src[hf][:], ACT.Abs, scale=1.0 / WSCALE, bias=bias).then_inc(chain, 1)
        ins = nc.scalar.activation(keep["rel"][:, hf], src[hf][:], ACT.Relu, scale=1.0 / WSCALE, bias=bias)
        if taken is not None:
            ins.then_inc(taken, 1)
    act.wait_ge(chain, chain_at + KC)
    nc.scalar.activation(keep["zt"][:], keep["zt"][:], ACT.Exp, scale=-1.0).then_inc(chain, 1)
    act.wait_ge(chain, chain_at + (KC + 1))
    nc.scalar.activation(keep["zt"][:], keep["zt"][:], ACT.Ln, bias=1.0).then_inc(ln_done, 1)


def prologue(nc, io, keep, banks, ctx):
    def sb(name, shape, dt):
        return ctx.enter_context(nc.sbuf_tensor(name, shape, dt))

    def sem(name):
        return ctx.enter_context(nc.semaphore(name))

    GN = 2
    GW = GN * D
    NG = N // GN
    stB, stC = (keep["yall"][:, m:m + 2].rearrange("p a b c -> p (a b c)").rearrange(
        "p (r c m) -> p r c m", r=2, c=KC) for m in (0, 2))
    rows = keep["rows"]
    xall = keep["x"]
    xcur = sb("xcur", [P, 2, CT, D], F32)
    stWd = sb("stWd", [P, KC, D], F32)
    Wd = keep["Wd"]
    stWr = sb("stWr", [P, KC, E], F32)
    Wr = sb("Wr", [P, 2, KC, E], F16)
    brb = sb("brb", [P, E], F32)
    stats = sb("stats", [P, NT, 6], F32)
    mean = sb("mean", [P, NT], F32)
    rstd = sb("rstd", [P, NT], F32)
    va = sb("va", [P, NT], F32)
    vb = sb("vb", [P, NT], F32)
    ident, ident16 = keep["ident"], keep["ident16"]
    ones = sb("ones", [P, P], F16)
    tri = sb("tri", [P, P], F16)
    rev = sb("rev", [P, E], F32)
    thr = sb("thr", [P, MAXB], F32)
    blk = sb("blk", [P, NBLK], F32)
    one_r = sb("one_r", [P, NT * E], F32)
    zero = keep["yall"][:, NCH - 1, 0, 0:D]
    rel, zt, dcur = keep["rel"], keep["zt"], keep["dcur"]

    small_in = sem("small_in")
    wgrp_in = [sem("wgrp_in0"), sem("wgrp_in1")]
    XP = 4
    x_in = [sem(f"x_in{k}") for k in range(XP)]
    consts = sem("consts")
    zero_set = sem("zero_set")
    b_hi = sem("b_hi")
    b_lo = sem("b_lo")
    c_hi = sem("c_hi")
    c_lo = sem("c_lo")
    wd_hi = sem("wd_hi")
    wd_lo = sem("wd_lo")
    stat_chain = sem("stat_chain")
    act_chain = sem("act_chain")
    var_ready = sem("var_ready")
    std_ready = sem("std_ready")
    xn_ready = sem("xn_ready")
    row_hi = sem("row_hi")
    row_lo = sem("row_lo")
    c_scaled = sem("c_scaled")
    xt_ready = sem("xt_ready")
    xt_done = [sem("xt_done_act"), sem("xt_done_dve")]
    gap_ready = sem("gap_ready")
    gap_exp = sem("gap_exp")
    cnt_ready = sem("cnt_ready")
    cnt_sum = sem("cnt_sum")
    sc_ready = sem("sc_ready")
    z_ready = sem("z_ready")
    z_chain = sem("z_chain")
    ln_ready = sem("ln_ready")
    delta_ready = sem("delta_ready")

    wb_v = io["WBT"].rearrange("(c p) m -> p c m", p=P)
    wc_v = io["WCT"].rearrange("(c p) m -> p c m", p=P)
    WB = keep["WB"][:].rearrange("p h c n d -> p h c (n d)")
    WC = keep["WC"][:].rearrange("p h c n d -> p h c (n d)")
    xT = keep["xT"]

    def router_sb(name):
        return sb(name, [P, NT, E], F32)

    sc, oh1, oh2, tmp = router_sb("sc"), router_sb("oh1"), router_sb("oh2"), router_sb("tmp")
    mx = sb("mx", [P, 2, NT], F32)
    top = sb("top", [P, NT], F32)
    M = sb("M", [P, E, NT], F32)
    cs = sb("cs", [P, E, NT], F32)
    rowc = sb("rowc", [P, E], F16)
    before = sb("before", [P, E], F32)
    nblk = sb("nblk", [P, E], F32)
    endb = sb("endb", [P, E], F32)
    off = sb("off", [P, E], F32)
    cmpb = sb("cmpb", [P, E, MAXB], F32)
    cmpe = sb("cmpe", [P, NBLK, E], F32)
    slotf = sb("slotf", [P, 2, NT], F32)
    ebf = sb("ebf", [P, NBLK], F32)

    def xt_at(part, kc, i, par, lo=0, n=CH):
        return xT[:, bass.ds(i * 2 + par, 1), part, kc, lo:lo + n].squeeze(1)

    def row_at(part, i, par):
        return rows[:, bass.ds(i * (2 * CT) + par * CT, CT), part, :]

    def turned_parts(par, kc):
        return banks[par * KC + kc][:].bitcast(F16).rearrange("p (b t) -> p b t", b=2)

    block = ctx.enter_context(nc.Block())

    @block.sync
    def _(sp):
        for k in range(XP):
            tiles = slice(k * NT // XP, (k + 1) * NT // XP)
            sp.dma_start(xall[:, tiles, :], io["x_tok"][:, tiles, :]).then_inc(x_in[k], 16)
        sp.dma_start(stWd[:], io["WdT"].rearrange("(c p) m -> p c m", p=P)).then_inc(small_in, 16)
        sp.dma_start(stWr[:], io["Wr"].rearrange("(c p) m -> p c m", p=P)).then_inc(small_in, 16)
        sp.dma_start(brb[:], io["br"].partition_broadcast(P)).then_inc(small_in, 16)
        sp.dma_start(keep["A"][:], io["A"].rearrange("(h p) n -> p h n", p=P)).then_inc(small_in, 16)
        sp.dma_start(keep["dbias"][:], io["dbias"]).then_inc(small_in, 16)
        with sp.Fori(0, NG // 2) as i:
            for par in range(2):
                sp.wait_ge(b_lo, i * 2 + (par + 1))
                sp.wait_ge(c_lo, i * 2 + (par + 1))
                at = i * (2 * GW) + par * GW
                sp.dma_start(stB[:, par], wb_v[:, :, bass.ds(at, GW)]).then_inc(wgrp_in[par], 16)
                sp.dma_start(stC[:, par], wc_v[:, :, bass.ds(at, GW)]).then_inc(wgrp_in[par], 16)
        sp.wait_ge(zero_set, 1)
        sp.dma_start(io["xs"].rearrange("(p r) d -> p r d", p=P),
                     zero.bitcast(F16).unsqueeze(1).broadcast_to([P, NSLOT // P, 2 * D])).then_inc(keep["zeros_out"], 16)

    @block.gpsimd
    def _(pool):
        pool.sem_inc(c_lo, 2)
        nc.gpsimd.memset(zero, 0.0).then_inc(zero_set, 1)
        nc.gpsimd.memset(ident[:], 0.0)
        nc.gpsimd.memset(tri[:], 1.0)
        nc.gpsimd.memset(ones[:], 1.0)
        nc.gpsimd.memset(one_r[:], 1.0).then_inc(consts, 1)
        pool.wait_ge(consts, 1)
        nc.gpsimd.affine_select(out=ident[:], in_=ident[:], compare_op=ALU.not_equal, fill=1.0, base=0,
                                pattern=[[-1, P]], channel_multiplier=1)
        nc.gpsimd.affine_select(out=tri[:], in_=tri[:], compare_op=ALU.is_gt, fill=0.0, base=0,
                                pattern=[[1, P]], channel_multiplier=-1)
        nc.gpsimd.iota(rev[:], pattern=[[-1, E]], base=E, channel_multiplier=0,
                       allow_small_or_imprecise_dtypes=True)
        nc.gpsimd.iota(thr[:], pattern=[[BT, MAXB]], base=0, channel_multiplier=0,
                       allow_small_or_imprecise_dtypes=True)
        nc.gpsimd.iota(blk[:], pattern=[[1, NBLK]], base=0, channel_multiplier=0,
                       allow_small_or_imprecise_dtypes=True).then_inc(consts, 1)
        pool.wait_ge(consts, 2)
        nc.gpsimd.tensor_copy(ident16[:], ident[:]).then_inc(consts, 1)
        with pool.Fori(0, NG // 2) as i:
            for par in range(2):
                pool.wait_ge(c_hi, i * 2 + (par + 1))
                at = i * (2 * GW) + par * GW
                nc.gpsimd.tensor_tensor(WC[:, 1, :, bass.ds(at, GW)], stC[:, par], WC[:, 0, :, bass.ds(at, GW)],
                                        ALU.subtract).then_inc(c_lo, 1)
        pool.wait_ge(ln_ready, 1)
        nc.gpsimd.tensor_tensor(dcur[:, 0], rel[:, 0], zt[:, 0], ALU.add).then_inc(delta_ready, 1)
        pool.wait_ge(delta_ready, 1)

    @block.scalar
    def _(act):
        act.wait_ge(small_in, 80)
        nc.scalar.activation(stWd[:], stWd[:], ACT.Copy, scale=WSCALE).then_inc(act_chain, 1)
        nc.scalar.activation(stWr[:], stWr[:], ACT.Copy, scale=WSCALE).then_inc(act_chain, 1)
        act.wait_ge(act_chain, 2)
        nc.scalar.activation(Wd[:, 0], stWd[:], ACT.Copy).then_inc(wd_hi, 1)
        nc.scalar.activation(Wr[:, 0], stWr[:], ACT.Copy).then_inc(wd_hi, 1)
        act.wait_ge(var_ready, 1)
        nc.scalar.activation(va[:], vb[:], ACT.Sqrt).then_inc(std_ready, 1)

        def weight_group(i, par):
            at = i * (2 * GW) + par * GW
            act.wait_ge(wgrp_in[par], i * 32 + 32)
            nc.scalar.activation(stC[:, par], stC[:, par], ACT.Copy, scale=WSCALE).then_inc(c_scaled, 1)
            nc.scalar.activation(WB[:, 0, :, bass.ds(at, GW)], stB[:, par], ACT.Copy, scale=WSCALE).then_inc(b_hi, 1)
            act.wait_ge(c_scaled, i * 2 + (par + 1))
            nc.scalar.activation(WC[:, 0, :, bass.ds(at, GW)], stC[:, par], ACT.Copy).then_inc(c_hi, 1)

        act.sem_inc(xt_done[0], 2)
        with act.Fori(0, NCH // 2) as i:
            for par in range(2):
                act.wait_ge(xn_ready, i * 2 + (par + 1))
                nc.scalar.activation(row_at(0, i, par), xcur[:, par], ACT.Copy).then_inc(row_hi, 1)
            for par in range(2):
                weight_group(i, par)
            for par in range(2):
                act.wait_ge(xt_ready, i * (2 * KC) + (par * KC + 1))
                nc.scalar.activation(xt_at(slice(0, 2), 0, i, par), turned_parts(par, 0), ACT.Copy).then_inc(xt_done[0], 1)
        softplus_parts(nc, act, keep, banks[4:6], z_ready, 1, z_chain, 0, None, ln_ready)
        act.wait_ge(gap_ready, 1)
        nc.scalar.activation(keep["w"][:, 1, :], keep["w"][:, 0, :], ACT.Exp).then_inc(gap_exp, 1)

    @block.vector
    def _(dve):
        v = nc.vector
        dve.sem_inc(row_lo, 2)
        dve.sem_inc(b_lo, 2)
        dve.sem_inc(xt_done[1], 2)
        for k in range(XP):
            dve.wait_ge(x_in[k], 16)
            with dve.Fori(k * NT // XP // 4, (k + 1) * NT // XP // 4) as i:
                for q in range(4):
                    one = bass.ds(i * 4 + q, 1)
                    v.bn_stats(stats[:, one, :].rearrange("p a b -> p (a b)"),
                               xall[:, one, :].rearrange("p a b -> p (a b)")).then_inc(stat_chain, 1)
        ch = Chain(dve, stat_chain)
        ch.n = NT
        dve.wait_ge(stat_chain, ch.n)
        m_e, q_e, m_o, q_o = stats[:, :, 1], stats[:, :, 2], stats[:, :, 4], stats[:, :, 5]
        ch.run(v.tensor_tensor(mean[:], m_e, m_o, ALU.add))
        ch.run(v.tensor_scalar(mean[:], mean[:], 0.5, None, ALU.mult))
        ch.run(v.tensor_tensor(va[:], m_e, m_o, ALU.subtract))
        ch.run(v.scalar_tensor_tensor(va[:], va[:], 0.25, va[:], ALU.mult, ALU.mult))
        ch.run(v.tensor_tensor(vb[:], q_e, q_o, ALU.add))
        ch.run(v.scalar_tensor_tensor(vb[:], vb[:], 1.0 / D, va[:], ALU.mult, ALU.add))
        ch.run(v.tensor_scalar(vb[:], vb[:], EPS, None, ALU.add))
        dve.sem_inc(var_ready, 1)
        dve.wait_ge(std_ready, 1)
        ch.run(v.reciprocal(rstd[:], va[:]))
        ch.run(v.tensor_tensor(va[:], rstd[:], rstd[:], ALU.mult))
        ch.run(v.tensor_tensor(va[:], va[:], vb[:], ALU.mult))
        ch.run(v.tensor_scalar(va[:], va[:], -0.5, 1.5, ALU.mult, ALU.add))
        ch.run(v.tensor_tensor(rstd[:], rstd[:], va[:], ALU.mult))
        dve.wait_ge(wd_hi, 2)
        v.reciprocal(keep["rA"][:], keep["A"][:])
        v.tensor_tensor(Wd[:, 1], stWd[:], Wd[:, 0], ALU.subtract).then_inc(wd_lo, 1)
        v.tensor_tensor(Wr[:, 1], stWr[:], Wr[:, 0], ALU.subtract).then_inc(wd_lo, 1)
        with dve.Fori(0, NCH // 2) as i:
            for par in range(2):
                dve.wait_ge(row_lo, i * 2 + (par + 1))
                for q in range(CT):
                    t = i * (2 * CT) + (par * CT + q)
                    ins = v.tensor_scalar(xcur[:, par, q, :], xall[:, bass.ds(t, 1), :].rearrange("p a b -> p (a b)"),
                                          mean[:, bass.ds(t, 1)], rstd[:, bass.ds(t, 1)],
                                          ALU.subtract, ALU.mult)
                ins.then_inc(xn_ready, 1)
            for par in range(2):
                dve.wait_ge(row_hi, i * 2 + (par + 1))
                v.tensor_tensor(row_at(1, i, par), xcur[:, par], row_at(0, i, par), ALU.subtract).then_inc(row_lo, 1)
            for par in range(2):
                at = i * (2 * GW) + par * GW
                dve.wait_ge(b_hi, i * 2 + (par + 1))
                v.scalar_tensor_tensor(WB[:, 1, :, bass.ds(at, GW)], stB[:, par], WSCALE, WB[:, 0, :, bass.ds(at, GW)],
                                       ALU.mult, ALU.subtract).then_inc(b_lo, 1)
            for par in range(2):
                dve.wait_ge(xt_ready, i * (2 * KC) + (par * KC + 2))
                v.tensor_scalar(xt_at(slice(0, 2), 1, i, par), turned_parts(par, 1), 1.0, None,
                                ALU.mult).then_inc(xt_done[1], 1)

        dve.wait_ge(sc_ready, NCH)
        dve.wait_ge(consts, 2)

        def per_token(ap):
            return ap.unsqueeze(2).broadcast_to([P, NT, E])

        def per_expert(ap):
            return ap.unsqueeze(1).broadcast_to([P, NT, E])

        sc_ps = banks[6][:, 0:NT * E].rearrange("p (i e) -> p i e", e=E)
        ch.run(v.scalar_tensor_tensor(sc[:], sc_ps, 1.0 / WSCALE, per_expert(brb[:]), ALU.mult, ALU.add))
        for k, oh in ((0, oh1), (1, oh2)):
            ch.run(v.tensor_reduce(mx[:, k, :], sc[:], AX.X, ALU.max))
            ch.run(v.tensor_tensor(tmp[:], sc[:], per_token(mx[:, k, :]), ALU.is_equal))
            ch.run(v.tensor_tensor(tmp[:], tmp[:], per_expert(rev[:]), ALU.mult))
            ch.run(v.tensor_reduce(top[:], tmp[:], AX.X, ALU.max))
            ch.run(v.tensor_tensor(oh[:], per_expert(rev[:]), per_token(top[:]), ALU.is_equal))
            if k == 0:
                ch.run(v.scalar_tensor_tensor(sc[:], oh[:], -BIG, sc[:], ALU.mult, ALU.add))
        ch.run(v.tensor_tensor(keep["w"][:, 0, :], mx[:, 1, :], mx[:, 0, :], ALU.subtract))
        dve.sem_inc(gap_ready, 1)
        ch.run(v.tensor_tensor(M[:].rearrange("p e i -> p i e"), oh1[:], oh2[:], ALU.add))
        ch.run(v.tensor_tensor_scan(cs[:].rearrange("p e i -> p (e i)"), one_r[:], M[:].rearrange("p e i -> p (e i)"),
                                    0.0, ALU.mult, ALU.add))
        last = cs[:, :, NT - 1]
        ch.run(v.memset(before[:, 0:1], 0.0))
        ch.run(v.tensor_copy(before[:, 1:E], cs[:, 0:E - 1, NT - 1]))
        ch.run(v.tensor_tensor(rowc[:], last, before[:], ALU.subtract))
        dve.sem_inc(cnt_ready, 1)
        ch.run(v.tensor_tensor(cs[:], cs[:], M[:], ALU.subtract))
        dve.wait_ge(cnt_sum, 1)
        earlier, total = banks[7][:, 0:E], banks[7][:, E:2 * E]
        ch.run(v.tensor_tensor(cmpb[:], total.unsqueeze(2).broadcast_to([P, E, MAXB]),
                               thr[:].unsqueeze(1).broadcast_to([P, E, MAXB]), ALU.is_gt))
        ch.run(v.tensor_reduce(nblk[:], cmpb[:], AX.X, ALU.add))
        ch.run(v.tensor_tensor_scan(endb[:], one_r[:, 0:E], nblk[:], 0.0, ALU.mult, ALU.add))
        ch.run(v.tensor_tensor(off[:], endb[:], nblk[:], ALU.subtract))
        ch.run(v.scalar_tensor_tensor(off[:], off[:], float(BT), earlier, ALU.mult, ALU.add))
        ch.run(v.tensor_tensor(off[:], off[:], before[:], ALU.subtract))
        ch.run(v.tensor_tensor(cs[:], cs[:], off[:].unsqueeze(2).broadcast_to([P, E, NT]), ALU.add))
        for k, oh in ((0, oh1), (1, oh2)):
            ch.run(v.tensor_tensor(tmp[:], oh[:], cs[:].rearrange("p e i -> p i e"), ALU.mult))
            ch.run(v.tensor_reduce(slotf[:, k, :], tmp[:], AX.X, ALU.add))
        ch.run(v.tensor_copy(keep["slot"][:], slotf[:]))
        ch.run(v.tensor_tensor(cmpe[:], endb[:].unsqueeze(1).broadcast_to([P, NBLK, E]),
                               blk[:].unsqueeze(2).broadcast_to([P, NBLK, E]), ALU.is_le))
        ch.run(v.tensor_reduce(ebf[:], cmpe[:], AX.X, ALU.add))
        ch.run(v.tensor_scalar(keep["eblk"][:], ebf[:], float(E - 1), None, ALU.min))
        dve.wait_ge(gap_exp, 1)
        ch.run(v.tensor_scalar(top[:], keep["w"][:, 1, :], 1.0, None, ALU.add))
        ch.run(v.reciprocal(keep["w"][:, 0, :], top[:]))
        ch.run(v.tensor_tensor(keep["w"][:, 1, :], keep["w"][:, 1, :], keep["w"][:, 0, :], ALU.mult))

    @block.tensor
    def _(pe):
        mm = nc.tensor.matmul
        pe.wait_ge(consts, 3)
        pe.wait_ge(wd_lo, 2)
        with pe.Fori(0, NCH // 2) as i:
            for par in range(2):
                pe.wait_ge(row_lo, i * 2 + (par + 1 + 2))
                for done in xt_done:
                    pe.wait_ge(done, i * 2 + (par + 1))
                for kc in range(KC):
                    for b in range(2):
                        for q in range(CT):
                            t = bass.ds(i * (2 * CT) + (par * CT + q), 1)
                            ins = nc.tensor.transpose(turned_parts(par, kc)[:, b, q * P:(q + 1) * P],
                                                      rows[:, t, b, kc * P:(kc + 1) * P].squeeze(1), ident16[:])
                    ins.then_inc(xt_ready, 1)
            for par in range(2):
                for done in xt_done:
                    pe.wait_ge(done, i * 2 + (par + 1 + 2))
                for q in range(CT):
                    n = 0
                    for kc in range(KC):
                        for a, b in ((0, 0), (0, 1), (1, 0), (1, 1)):
                            n += 1
                            ins = mm(banks[6][:, bass.ds(i * (2 * CT * E) + (par * CT + q) * E, E)],
                                     xt_at(a, kc, i, par, q * P, P), Wr[:, b, kc, :],
                                     start=(n == 1), stop=(n == 4 * KC))
                ins.then_inc(sc_ready, 1)
        project_z(nc, keep, banks[4:6], 0, z_ready)
        pe.wait_ge(cnt_ready, 1)
        mm(banks[7][:, 0:E], tri[:], rowc[:], start=True, stop=True)
        mm(banks[7][:, E:2 * E], ones[:], rowc[:], start=True, stop=True).then_inc(cnt_sum, 1)


def scan_phase(nc, io, keep, banks, ctx, row):
    split_weights, combine = row == 0, row == 1

    def sb(name, shape, dt):
        return ctx.enter_context(nc.sbuf_tensor(f"{name}_{row}", shape, dt))

    def sem(name):
        return ctx.enter_context(nc.semaphore(f"{name}_{row}"))

    AR = 4
    aexp = sb("aexp", [P, AR, CH], F32)
    ub = sb("ub", [P, 2, CH], F32)
    uxb = sb("uxb", [P, 2, CH], F32)
    hb = sb("hb", [P, AR, CH], F32)
    hcb = sb("hcb", [P, 2, CH], F32)
    x32 = sb("x32", [P, KC, CH], F32)
    state = sb("state", [P, TILES], F32)
    Bps, Cps, Yps, Ops = banks[0:2], banks[2:4], banks[4:6], banks[6:8]
    xT, WB, WC, A = keep["xT"], keep["WB"], keep["WC"], keep["A"]
    rel, zt, dcur, yall = keep["rel"], keep["zt"], keep["dcur"], keep["yall"]

    a_ready = sem("a_ready")
    B_ready = sem("B_ready")
    C_ready = sem("C_ready")
    u_done = sem("u_done")
    ux_done = sem("ux_done")
    h_done = sem("h_done")
    hc_done = sem("hc_done")
    acc_done = sem("acc_done")
    state_saved = sem("state_saved")
    x32_done = sem("x32_done")
    z_ready = sem("z_ready")
    z_taken = sem("z_taken")
    z_chain = sem("z_chain")
    ln_done = sem("ln_done")
    delta_done = sem("delta_done")
    U_CR, UX_CR, H_CR, HC_CR, ACC_CR, ST_CR, D_CR = 2, 1, AR, 2, 1, AR, 1
    ACCS = TILES - KC
    Z_AT, Z_LOG, D_NEXT, D_HERE = 3, 6, 20, 2

    if split_weights:
        stage = yall[:, RCH:NCH].rearrange("p a b c -> p (a b c)")
        wst = stage[:, 0:2 * PIECE].rearrange("p (r f) -> p r f", r=2)
        whl = stage[:, 2 * PIECE:4 * PIECE].bitcast(F16).rearrange("p (r h f) -> p r h f", r=2, h=2)
        piece_in = [sem("piece_in0"), sem("piece_in1")]
        piece_out = [sem("piece_out0"), sem("piece_out1")]
        p_scaled = sem("p_scaled")
        p_hi = sem("p_hi")
        p_lo = sem("p_lo")
    if combine:
        gat = xT[:, 0:RCH].rearrange("p a b c d -> p (a b c d)").bitcast(F32).rearrange(
            "p (g q k d) -> p g q k d", g=2, q=CT, k=2)
        ycur = sb("ycur", [P, 2, KC, CH], F32)
        xres = sb("xres", [P, 2, CT, D], F32)
        ob = sb("ob", [P, 2, CT, D], F32)
        sidx = sb("sidx", [P, 2, 2, CT], U32)
        ycur_done = sem("ycur_done")
        idx_done = sem("idx_done")
        turned = sem("turned")
        gathered = [sem("gathered0"), sem("gathered1")]
        xres_in = [sem("xres_in0"), sem("xres_in1")]
        weighted = [sem("weighted0"), sem("weighted1")]
        experts_added = [sem("experts_added0"), sem("experts_added1")]
        x_added = [sem("x_added0"), sem("x_added1")]
        o_ready = sem("o_ready")
        out_sent = [sem("out_sent0"), sem("out_sent1")]
    GATHER_AT, WEIGH_AT, ADD_AT, TURN_AT, CLOSE_AT = (0, 8), (10, 19), (15, 24), (8, 22), (19, 28)

    def tile(s):
        return s // N, s % N

    def chunk(t, c):
        return t[:, bass.ds(c + row * RCH, 1)].squeeze(1)

    def group_chunk(c, g, last):
        return NCH - 1 if last and g == 0 else c + 3 * g

    def group_at(c, g, last):
        return c * 2 + (1 - g if last else g)

    def group_tiles(c, g, last):
        return bass.ds(group_chunk(c, g, last) * CT, CT)

    def chunks(eng, body):
        if combine:
            with eng.Fori(0, RCH - 1) as c:
                body(c, False)
            body(RCH - 1, True)
        else:
            with eng.Fori(0, RCH) as c:
                body(c, False)

    PIECES = E * NPIECE // RCH
    EPC = E // RCH
    STRIDE = 3

    def store_piece(sp, c, k):
        ex = c * EPC + k // NPIECE
        sp.wait_ge(p_lo, c * PIECES + (k + 1 + 2))
        sp.dma_start(io["wsplit"][bass.ds(ex, 1), :, k % NPIECE, :, :].rearrange("a p h f -> p (a h) f"),
                     whl[:, k % 2]).then_inc(piece_out[k % 2], 16)

    block = ctx.enter_context(nc.Block())

    @block.sync
    def _(sp):
        if split_weights:
            with sp.Fori(0, RCH) as c:
                for k in range(PIECES):
                    par = k % 2
                    ex = c * EPC + k // NPIECE
                    pc = k % NPIECE
                    sp.wait_ge(p_lo, c * PIECES + (k + 1))
                    if pc < KC:
                        src = io["W1"][bass.ds(ex, 1), pc * P:(pc + 1) * P, :].rearrange("a p f -> p (a f)")
                        sp.dma_start(wst[:, par, :], src).then_inc(piece_in[par], 16)
                    else:
                        fc = (pc - KC) * (FC // 2)
                        src = io["W2"][bass.ds(ex, 1), fc * P:(fc + FC // 2) * P, :]\
                            .rearrange("a (c p) d -> p (a c) d", p=P)
                        sp.dma_start(wst[:, par, :].rearrange("p (c d) -> p c d", d=D), src).then_inc(piece_in[par], 16)
                    if k >= 1:
                        store_piece(sp, c, k - 1)
                store_piece(sp, c, PIECES - 1)
            for par in range(2):
                sp.wait_ge(piece_out[par], (RCH * PIECES // 2 + 1) * 16)

        def body(c, last):
            order = (1, 0) if last else (0, 1)
            for g in order:
                sp.wait_ge(o_ready, c * 2 + (g + 1))
                sp.dma_start(xres[:, g], io["x_tok"][:, group_tiles(c, g, last), :]).then_inc(xres_in[g], 16)
            for g in order:
                sp.wait_ge(o_ready, group_at(c, g, last) + 3)
                sp.dma_start(io["out_tok"][:, group_tiles(c, g, last), :], ob[:, g]).then_inc(out_sent[g], 16)

        if combine:
            chunks(sp, body)
            for g in range(2):
                sp.wait_ge(out_sent[g], (RCH + 1) * 16)

    @block.scalar
    def _(act):
        act.sem_inc(state_saved, ST_CR)
        if split_weights:
            act.wait_ge(keep["zeros_out"], 16)
        act.sem_inc(z_taken, KC)

        def save_state(c, s):
            act.wait_ge(h_done, c * TILES + (s + 1 + H_CR))
            nc.scalar.activation(state[:, s:s + 1], hb[:, s % AR, CH - 1:CH], ACT.Copy).then_inc(state_saved, 1)

        def body(c, last):
            for s in range(TILES):
                hf, n = tile(s)
                if n == 0:
                    act.wait_ge(delta_done, c * 2 + (hf + 1))
                act.wait_ge(h_done, c * TILES + (s + 1))
                nc.scalar.activation(aexp[:, s % AR], dcur[:, hf, :], ACT.Exp,
                                     scale=A[:, hf, n:n + 1]).then_inc(a_ready, 1)
                if s >= 3:
                    save_state(c, s - 3)
                if s == Z_LOG and not last:
                    act.wait_ge(delta_done, c * 2 + 2)
                    softplus_parts(nc, act, keep, Ops, z_ready, c + 1, z_chain, c * (KC + 1), z_taken, ln_done)
                if split_weights and s % STRIDE == 1 and s // STRIDE < PIECES:
                    k = s // STRIDE
                    par = k % 2
                    act.wait_ge(piece_in[par], (c * (PIECES // 2) + (k // 2 + 1)) * 16)
                    nc.scalar.activation(wst[:, par, :], wst[:, par, :], ACT.Copy, scale=WSCALE).then_inc(p_scaled, 1)
                    act.wait_ge(piece_out[par], (c * (PIECES // 2) + (k // 2 + 1)) * 16)
                    act.wait_ge(p_scaled, c * PIECES + (k + 1))
                    nc.scalar.activation(whl[:, par, 0, :], wst[:, par, :], ACT.Copy).then_inc(p_hi, 1)
                if combine and s in (5, 19) and not (last and s == 5):
                    take_y(c, s // 19, last)
                for g in range(2) if combine else ():
                    if WEIGH_AT[g] <= s < WEIGH_AT[g] + CT:
                        weigh(c, g, s - WEIGH_AT[g], last)
            for s in range(TILES - 3, TILES):
                save_state(c, s)
            if last:
                take_y(c, 0, last)

        def weigh(c, g, q, last):
            tok = bass.ds(group_chunk(c, g, last) * CT + q, 1)
            if q == 0:
                act.wait_ge(gathered[g], c * (2 * CT * 16) + 2 * CT * 16)
            for k in range(2):
                ins = nc.scalar.activation(gat[:, g, q, k], gat[:, g, q, k], ACT.Copy, scale=keep["w"][:, k, tok])
            if q == CT - 1:
                ins.then_inc(weighted[g], 1)

        def take_y(c, g, last):
            act.wait_ge(acc_done, (c + (1 if last and g == 0 else 0)) * ACCS + 1)
            act.wait_ge(turned, group_at(c, g, last) + 1)
            nc.scalar.activation(ycur[:, g], yall[:, bass.ds(group_chunk(c, g, last), 1)].squeeze(1), ACT.Copy,
                                 scale=1.0 / (WSCALE * WSCALE)).then_inc(ycur_done, 1)

        chunks(act, body)

    @block.gpsimd
    def _(pool):
        pool.sem_inc(ux_done, UX_CR)
        pool.sem_inc(delta_done, D_CR)
        if split_weights:
            pool.sem_inc(p_lo, 2)
            pool.sem_inc(piece_out[0], 16)
            pool.sem_inc(piece_out[1], 16)
            pool.wait_ge(keep["zeros_out"], 16)
        if combine:
            pool.sem_inc(out_sent[0], 16)
            pool.sem_inc(out_sent[1], 16)
            for k in range(2):
                pool.wait_ge(keep["y_out"][k], (NBLK // 2 + 2 - k) * 16)

        def body(c, last, scatter=()):
            pool.wait_ge(ux_done, c * TILES + 1)
            nc.gpsimd.tensor_tensor(x32[:], chunk(xT, c)[:, 0], chunk(xT, c)[:, 1], ALU.add).then_inc(x32_done, 1)
            pool.wait_ge(x32_done, c + 1)
            if combine:
                for g in range(2):
                    ins = nc.gpsimd.tensor_copy(sidx[:, g], keep["slot"][:, :, group_tiles(c, g, last)])
                ins.then_inc(idx_done, 1)
                pool.wait_ge(idx_done, c + 1)
            for s in range(TILES):
                hf, n = tile(s)
                pool.wait_ge(u_done, c * TILES + (s + 1 + U_CR))
                pool.wait_ge(h_done, c * TILES + (s + AR - 1))
                nc.gpsimd.tensor_tensor(uxb[:, s % 2], ub[:, s % 2], x32[:, hf], ALU.mult).then_inc(ux_done, 1)
                if s == D_HERE:
                    pool.wait_ge(a_ready, c * TILES + 1)
                    nc.gpsimd.tensor_tensor(dcur[:, 1], rel[:, 1], zt[:, 1], ALU.add).then_inc(delta_done, 1)
                if s == D_NEXT and not last:
                    pool.wait_ge(a_ready, c * TILES + N)
                    pool.wait_ge(ln_done, c + 1)
                    nc.gpsimd.tensor_tensor(dcur[:, 0], rel[:, 0], zt[:, 0], ALU.add).then_inc(delta_done, 1)
                if split_weights and s % STRIDE == 2 and s // STRIDE < PIECES:
                    k = s // STRIDE
                    par = k % 2
                    pool.wait_ge(p_hi, c * PIECES + (k + 1))
                    nc.gpsimd.tensor_tensor(whl[:, par, 1, :], wst[:, par, :], whl[:, par, 0, :],
                                            ALU.subtract).then_inc(p_lo, 1)
                for i, k in scatter[s // 2:s // 2 + 1] if s % 2 == 0 else ():
                    nc.gpsimd.indirect_dma_start(
                        out=io["xs"], out_offset=bass.IndirectOffsetOnAxis(keep["slot"][:, k, i:i + 1], 0),
                        in_=keep["rows"][:, i].rearrange("p a d -> p (a d)"), in_offset=None).then_inc(keep["scattered"], 16)
                for g in range(2) if combine else ():
                    if s == ADD_AT[g]:
                        pool.wait_ge(weighted[g], c + 1)
                        pool.wait_ge(out_sent[g], c * 16 + 16)
                        nc.gpsimd.tensor_tensor(ob[:, g], gat[:, g, :, 0], gat[:, g, :, 1],
                                                ALU.add).then_inc(experts_added[g], 1)
                    if s == ADD_AT[g] + 2:
                        pool.wait_ge(experts_added[g], c + 1)
                        pool.wait_ge(xres_in[g], c * 16 + 16)
                        nc.gpsimd.tensor_tensor(ob[:, g], ob[:, g], xres[:, g], ALU.add).then_inc(x_added[g], 1)
                if combine and s < 4 * CT:
                    g, q, k = s // (2 * CT), s % (2 * CT) // 2, s % 2
                    nc.gpsimd.indirect_dma_start(
                        out=gat[:, g, q, k, :], out_offset=None, in_=io["ys"],
                        in_offset=bass.IndirectOffsetOnAxis(sidx[:, g, k, q:q + 1], 0)).then_inc(gathered[g], 16)

        if split_weights:
            todo = [(i, k) for i in range(NT) for k in range(2)]
            for c in range(RCH):
                body(c, False, todo[c * len(todo) // RCH:(c + 1) * len(todo) // RCH])
            pool.wait_ge(keep["scattered"], len(todo) * 16)
        else:
            chunks(pool, body)

    @block.vector
    def _(dve):
        v = nc.vector
        dve.sem_inc(u_done, U_CR)
        dve.sem_inc(h_done, H_CR)
        dve.sem_inc(hc_done, HC_CR)
        dve.sem_inc(acc_done, ACC_CR)
        if combine:
            dve.sem_inc(o_ready, 2)
        v.memset(state[:], 0.0)

        def u_op(c, s):
            dve.wait_ge(a_ready, c * TILES + (s + 1))
            dve.wait_ge(B_ready, c * TILES + (s + 1))
            v.scalar_tensor_tensor(ub[:, s % 2], aexp[:, s % AR], -1.0, Bps[s % 2][:], ALU.add,
                                   ALU.mult).then_inc(u_done, 1)

        def scan_op(c, s):
            dve.wait_ge(ux_done, c * TILES + (s + 1 + UX_CR))
            dve.wait_ge(state_saved, c * TILES + (s + 1))
            v.tensor_tensor_scan(hb[:, s % AR], aexp[:, s % AR], uxb[:, s % 2], state[:, s:s + 1],
                                 ALU.mult, ALU.add).then_inc(h_done, 1)

        def hc_op(c, s):
            hf, n = tile(s)
            dve.wait_ge(C_ready, c * TILES + (s + 1))
            dve.wait_ge(h_done, c * TILES + (s + 1 + H_CR))
            dst = Yps[hf][:] if n == 0 else hcb[:, s % 2]
            v.scalar_tensor_tensor(dst, hb[:, s % AR], keep["rA"][:, hf, n:n + 1], Cps[s % 2][:], ALU.mult,
                                   ALU.mult).then_inc(hc_done, 1)

        def acc_op(c, s):
            hf, n = tile(s)
            if n == 0:
                return
            dve.wait_ge(hc_done, c * TILES + (s + 1 + HC_CR))
            dve.wait_ge(acc_done, c * ACCS + (hf * (N - 1) + n - 1 + ACC_CR))
            dst = chunk(yall, c)[:, hf] if n == N - 1 else Yps[hf][:]
            v.tensor_tensor(dst, Yps[hf][:], hcb[:, s % 2], ALU.add).then_inc(acc_done, 1)

        def close_op(c, g, half, last):
            if half == 0:
                dve.wait_ge(x_added[g], c + 1)
                dve.wait_ge(turned, group_at(c, g, last) + 3)
            ins = v.tensor_tensor(ob[:, g, half * 2:half * 2 + 2], ob[:, g, half * 2:half * 2 + 2],
                                  Ops[half][:].rearrange("p (q d) -> p q d", q=2), ALU.add)
            if half == 1:
                ins.then_inc(o_ready, 1)

        def body(c, last):
            for s in range(TILES):
                u_op(c, s)
                if s >= 1:
                    scan_op(c, s - 1)
                if s >= 2:
                    acc_op(c, s - 2)
                if s >= 1:
                    hc_op(c, s - 1)
                for g in range(2) if combine else ():
                    if CLOSE_AT[g] <= s < CLOSE_AT[g] + 2 and not (last and g == 0):
                        close_op(c, g, s - CLOSE_AT[g], last)
            scan_op(c, TILES - 1)
            acc_op(c, TILES - 2)
            hc_op(c, TILES - 1)
            acc_op(c, TILES - 1)
            if last:
                for half in range(2):
                    close_op(c, 0, half, last)

        chunks(dve, body)

    @block.tensor
    def _(pe):
        mm = nc.tensor.matmul
        if combine:
            pe.sem_inc(turned, 2)

        def project(bank, W, c, s, done):
            hf, n = tile(s)
            k = 0
            for kc in range(KC):
                for a, b in ((0, 0), (0, 1), (1, 0)):
                    k += 1
                    ins = mm(bank[:], W[:, a, kc, n, hf * P:(hf + 1) * P], chunk(xT, c)[:, b, kc, :],
                             start=(k == 1), stop=(k == 3 * KC))
            ins.then_inc(done, 1)

        def project_c(c, s):
            pe.wait_ge(hc_done, c * TILES + (s + 1))
            project(Cps[s % 2], WC, c, s, C_ready)

        def turn(c, g, last):
            pe.wait_ge(ycur_done, group_at(c, g, last) + 1)
            pe.wait_ge(o_ready, group_at(c, g, last) + 2)
            pe.wait_ge(z_taken, (c + (0 if last else 1)) * KC + KC)
            for q in range(CT):
                for hf in range(KC):
                    col = q % 2 * D + hf * P
                    ins = nc.tensor.transpose(Ops[q // 2][:, col:col + P], ycur[:, g, hf, q * P:(q + 1) * P],
                                              keep["ident"][:])
            ins.then_inc(turned, 1)

        def body(c, last):
            for s in range(TILES):
                pe.wait_ge(u_done, c * TILES + (s + 1))
                project(Bps[s % 2], WB, c, s, B_ready)
                if s >= 1:
                    project_c(c, s - 1)
                if s == Z_AT and not last:
                    if combine:
                        pe.wait_ge(o_ready, c * 2 + 2)
                    pe.wait_ge(z_taken, c * KC + KC)
                    project_z(nc, keep, Ops, c + (row * RCH + 1), z_ready)
                if combine and s == TURN_AT[0] and not last:
                    turn(c, 0, last)
                if combine and s == TURN_AT[1]:
                    turn(c, 1, last)
            project_c(c, TILES - 1)
            if last:
                turn(c, 0, last)

        chunks(pe, body)


def expert_phase(nc, io, keep, banks, ctx):
    def sb(name, shape, dt):
        return ctx.enter_context(nc.sbuf_tensor(name, shape, dt))

    def sem(name):
        return ctx.enter_context(nc.semaphore(name))

    w1 = keep["xT"][:, 0:RCH].rearrange("p a b c d -> p (a b c d)").rearrange(
        "p (r c h f) -> p r c h f", r=2, c=KC, h=2)
    hs = sb("hs", [P, 2, 2, FC, BT], F16)
    w2 = sb("w2", [P, 2, 2, 2, FC // 2, D], F16)
    b1 = sb("b1", [P, 2, FC], F32)
    b2 = sb("b2", [P, 2, D], F32)
    xb = sb("xb", [P, 2, BS, 2 * D], F16)
    xbt = sb("xbt", [P, 2, 2, KC, BT], F16)
    h32 = sb("h32", [P, FC, BT], F32)
    yo = sb("yo", [P, 2, BS, D], F32)
    Hps, Tps, Yps = banks[0:4], banks[4:6], banks[6:8]

    w1_in = [sem("w1_in0"), sem("w1_in1")]
    w2_in = [sem("w2_in0"), sem("w2_in1")]
    xb_in = [sem("xb_in0"), sem("xb_in1")]
    y_out = keep["y_out"]
    T_done = sem("T_done")
    H_done = sem("H_done")
    Y_done = sem("Y_done")
    xbt_done = sem("xbt_done")
    gelu_done = sem("gelu_done")
    hhi_done = sem("hhi_done")
    hlo_done = sem("hlo_done")
    y_taken = sem("y_taken")
    PAIRS = FC // 2
    xs_v = io["xs"].rearrange("(b s p) d -> p b s d", s=BS, p=P)
    ys_v = io["ys"].rearrange("(b s p) d -> p b s d", s=BS, p=P)

    block = ctx.enter_context(nc.Block())


    @block.sync
    def _(sp):
        def load_slots(b, par):
            sp.wait_ge(T_done, b + 1)
            sp.dma_start(xb[:, par], xs_v[:, bass.ds(b, 1)].rearrange("p b s d -> p (b s) d")).then_inc(xb_in[par], 16)

        def load_w1(b, par):
            ex = sp.value_load(keep["eblk"][0:1, bass.ds(b, 1)], min_val=0, max_val=E - 1)
            sp.wait_ge(H_done, b * PAIRS + PAIRS)
            sp.wait_ge(gelu_done, b * FC + FC)
            sp.dma_start(w1[:, par], io["wsplit"][bass.ds(ex, 1), :, 0:KC].rearrange("a p c h f -> p (a c) h f"))\
                .then_inc(w1_in[par], 16)
            sp.dma_start(b1[:, par], io["b1"][bass.ds(ex, 1)].rearrange("a p c -> p (a c)")).then_inc(w1_in[par], 16)

        def store(b, par):
            sp.wait_ge(y_taken, b + (1 + 2))
            sp.dma_start(ys_v[:, bass.ds(b, 1)].rearrange("p b s d -> p (b s) d"), yo[:, par]).then_inc(y_out[par], 16)

        sp.sem_inc(y_out[0], 16)
        sp.sem_inc(y_out[1], 16)
        sp.wait_ge(keep["scattered"], 2 * NT * 16)
        load_slots(0, 0)
        load_w1(0, 0)
        load_slots(1, 1)
        load_w1(1, 1)
        load_slots(2, 0)
        load_w1(2, 0)
        load_slots(3, 1)
        with sp.Fori(0, (NBLK - 5) // 2) as i:
            for m in range(2):
                load_w1(i * 2 + (m + 3), (m + 1) % 2)
                load_slots(i * 2 + (m + 4), m)
                store(i * 2 + m, m)
        load_w1(NBLK - 2, 1)
        load_slots(NBLK - 1, 0)
        store(NBLK - 5, 0)
        load_w1(NBLK - 1, 0)
        for b in range(NBLK - 4, NBLK):
            store(b, b % 2)

    @block.gpsimd
    def _(pool):
        def load(b, par):
            ex = pool.value_load(keep["eblk"][0:1, bass.ds(b, 1)], min_val=0, max_val=E - 1)
            pool.wait_ge(y_taken, b + 1)
            pool.dma_start(w2[:, par].rearrange("p c h f d -> p c h (f d)"),
                           io["wsplit"][bass.ds(ex, 1), :, KC:NPIECE].rearrange("a p c h f -> p (a c) h f"))\
                .then_inc(w2_in[par], 16)
            pool.dma_start(b2[:, par], io["b2"][bass.ds(ex, 1), :].broadcast_to([P, D])).then_inc(w2_in[par], 16)

        pool.wait_ge(w1_in[0], 32)
        with pool.Fori(0, NBLK // 2) as i:
            for par in range(2):
                load(i * 2 + par, par)
        load(NBLK - 1, 0)

    @block.tensor
    def _(pe):
        mm = nc.tensor.matmul
        pe.sem_inc(T_done, 2)
        pe.sem_inc(H_done, 2 * PAIRS)
        pe.sem_inc(Y_done, 2)

        def turn(b, par, half):
            pe.wait_ge(xb_in[par], half * 16 + 16)
            pe.wait_ge(xbt_done, b + 1)
            for a in range(2):
                for kc in range(KC):
                    for s in range(BS):
                        ins = nc.tensor.transpose(Tps[par][:].bitcast(F16)[:, bass.ds(((a * KC + kc) * BS + s) * P, P)],
                                                  xb[:, par, s, bass.ds((a * KC + kc) * P, P)], keep["ident16"][:])
            ins.then_inc(T_done, 1)

        def hidden(b, par, half):
            pe.wait_ge(xbt_done, b + 1 + 2)
            pe.wait_ge(w1_in[par], half * 32 + 32)
            for fc in range(FC):
                if fc % 2 == 0:
                    pe.wait_ge(gelu_done, b * FC + (FC + fc + 2))
                k = 0
                for kc in range(KC):
                    for a, c in ((0, 0), (0, 1), (1, 0)):
                        k += 1
                        ins = mm(Hps[fc // 2][:, fc % 2 * BT:(fc % 2 + 1) * BT], w1[:, par, kc, a, fc * P:(fc + 1) * P],
                                 xbt[:, par, c, kc, :], start=(k == 1), stop=(k == 3 * KC))
                if fc % 2 == 1:
                    ins.then_inc(H_done, 1)

        def down(b, par, half):
            pe.wait_ge(w2_in[par], half * 32 + 32)
            pe.wait_ge(y_taken, b + 1)
            pe.wait_ge(hlo_done, b * 2 + 2 + 4)
            for s in range(BS):
                k = 0
                for fc in range(FC):
                    for a, c in ((0, 0), (0, 1), (1, 0)):
                        k += 1
                        ins = mm(Yps[par][:, s * D:(s + 1) * D], hs[:, par, a, fc, s * P:(s + 1) * P],
                                 w2[:, par, fc // (FC // 2), c, fc % (FC // 2), :],
                                 start=(k == 1), stop=(k == 3 * FC))
            ins.then_inc(Y_done, 1)

        turn(0, 0, 0)
        hidden(0, 0, 0)
        turn(1, 1, 0)
        with pe.Fori(0, NBLK // 2 - 1) as i:
            hidden(i * 2 + 1, 1, i)
            turn(i * 2 + 2, 0, i + 1)
            down(i * 2, 0, i)
            hidden(i * 2 + 2, 0, i + 1)
            turn(i * 2 + 3, 1, i + 1)
            down(i * 2 + 1, 1, i)
        hidden(NBLK - 2, 1, NBLK // 2 - 1)
        turn(NBLK - 1, 0, NBLK // 2)
        down(NBLK - 3, 0, NBLK // 2 - 1)
        hidden(NBLK - 1, 0, NBLK // 2)
        down(NBLK - 2, 1, NBLK // 2 - 1)
        down(NBLK - 1, 0, NBLK // 2)

    @block.scalar
    def _(act):
        act.sem_inc(gelu_done, 2 * FC)
        act.sem_inc(xbt_done, 2)

        def take_x(b, par):
            act.wait_ge(T_done, b + 1 + 2)
            act.wait_ge(H_done, b * PAIRS + PAIRS)
            nc.scalar.activation(xbt[:, par].rearrange("p a c s -> p (a c s)"), Tps[par][:].bitcast(F16),
                                 ACT.Copy).then_inc(xbt_done, 1)

        def gelus(b, par, half):
            act.wait_ge(w1_in[par], half * 32 + 32)
            for fc in range(FC):
                if fc % 2 == 0:
                    act.wait_ge(H_done, b * PAIRS + (fc // 2 + 1 + 2 * PAIRS))
                if fc % (FC // 2) == 0:
                    act.wait_ge(hlo_done, b * 2 + (fc // (FC // 2) + 1 + 2))
                nc.scalar.activation(h32[:, fc, :], Hps[fc // 2][:, fc % 2 * BT:(fc % 2 + 1) * BT],
                                     ACT.Gelu_apprx_tanh, bias=b1[:, par, fc:fc + 1],
                                     scale=1.0 / WSCALE).then_inc(gelu_done, 1)

        take_x(0, 0)
        with act.Fori(0, NBLK // 2) as i:
            gelus(i * 2, 0, i)
            take_x(i * 2 + 1, 1)
            gelus(i * 2 + 1, 1, i)
            take_x(i * 2 + 2, 0)
        gelus(NBLK - 1, 0, NBLK // 2)

    @block.vector
    def _(dve):
        v = nc.vector
        dve.sem_inc(hlo_done, 4)
        dve.sem_inc(y_taken, 2)

        def split_h(b, par):
            dve.wait_ge(Y_done, b + 1)
            for q in range(2):
                fs = slice(q * (FC // 2), (q + 1) * (FC // 2))
                dve.wait_ge(gelu_done, b * FC + ((q + 1) * (FC // 2) + 2 * FC))
                v.tensor_copy(hs[:, par, 0, fs, :], h32[:, fs, :]).then_inc(hhi_done, 1)
                dve.wait_ge(hhi_done, b * 2 + (q + 1))
                v.tensor_tensor(hs[:, par, 1, fs, :], h32[:, fs, :], hs[:, par, 0, fs, :],
                                ALU.subtract).then_inc(hlo_done, 1)

        def take_y(b, par, half):
            dve.wait_ge(Y_done, b + 1 + 2)
            dve.wait_ge(y_out[par], half * 16 + 16)
            v.scalar_tensor_tensor(yo[:, par], Yps[par][:].rearrange("p (s d) -> p s d", d=D), 1.0 / WSCALE,
                                   b2[:, par].unsqueeze(1).broadcast_to([P, BS, D]), ALU.mult,
                                   ALU.add).then_inc(y_taken, 1)

        split_h(0, 0)
        with dve.Fori(0, NBLK // 2 - 1) as i:
            split_h(i * 2 + 1, 1)
            take_y(i * 2, 0, i)
            split_h(i * 2 + 2, 0)
            take_y(i * 2 + 1, 1, i)
        split_h(NBLK - 2, 1)
        take_y(NBLK - 3, 0, NBLK // 2 - 1)
        split_h(NBLK - 1, 0)
        take_y(NBLK - 2, 1, NBLK // 2 - 1)
        take_y(NBLK - 1, 0, NBLK // 2)


def program(nc, io):
    io["xs"] = nc.dram_tensor("xs", [NSLOT, 2 * D], F16).ap()
    io["ys"] = nc.dram_tensor("ys", [NSLOT, D], F32).ap()
    io["wsplit"] = nc.dram_tensor("wsplit", [E, P, NPIECE, 2, PIECE], F16).ap()
    io["x_tok"] = io["x"].rearrange("b (i p) d -> p (b i) d", p=P)
    io["out_tok"] = io["out"].rearrange("b (i p) d -> p (b i) d", p=P)
    with ExitStack() as ctx:
        keep = {}

        def kp(name, shape, dt):
            keep[name] = ctx.enter_context(nc.sbuf_tensor(f"k_{name}", shape, dt))

        kp("WB", [P, 2, KC, N, D], F16)
        kp("WC", [P, 2, KC, N, D], F16)
        kp("xT", [P, NCH, 2, KC, CH], F16)
        kp("Wd", [P, 2, KC, D], F16)
        kp("rel", [P, KC, CH], F32)
        kp("zt", [P, KC, CH], F32)
        kp("dcur", [P, KC, CH], F32)
        kp("yall", [P, NCH, KC, CH], F32)
        kp("A", [P, KC, N], F32)
        kp("rA", [P, KC, N], F32)
        kp("dbias", [P, KC], F32)
        kp("ident", [P, P], F32)
        kp("ident16", [P, P], F16)
        kp("w", [P, 2, NT], F32)
        kp("slot", [P, 2, NT], U32)
        kp("eblk", [P, NBLK], I32)
        keep["scattered"] = ctx.enter_context(nc.semaphore("scattered"))
        keep["y_out"] = [ctx.enter_context(nc.semaphore(f"y_out{k}")) for k in range(2)]
        keep["zeros_out"] = ctx.enter_context(nc.semaphore("zeros_out"))
        banks = [ctx.enter_context(nc.psum_tensor(f"bank{i}", [P, 512], F32)) for i in range(8)]
        with ExitStack() as rows_ctx:
            keep["x"] = rows_ctx.enter_context(nc.sbuf_tensor("xrows", [P, NT, D], F32))
            keep["rows"] = keep["x"][:].bitcast(F16).rearrange("p t (a d) -> p t a d", a=2)
            with ExitStack() as c1:
                prologue(nc, io, keep, banks, c1)
            with ExitStack() as c1:
                scan_phase(nc, io, keep, banks, c1, 0)
        with ExitStack() as c1:
            expert_phase(nc, io, keep, banks, c1)
        with ExitStack() as c1:
            scan_phase(nc, io, keep, banks, c1, 1)


def kernel(**inputs):
    import numpy as np
    import concourse.bacc as bacc
    from concourse.bass_utils import run_bass_kernel_spmd

    a = {k: np.asarray(v) for k, v in inputs.items()}
    arrays = {
        "x": a["L0_attn_x"],
        "A": a["L0_attn_A"],
        "WdT": a["L0_attn_W_delta"].T,
        "dbias": a["L0_attn_delta_bias"].reshape(KC, P).T,
        "WBT": a["L0_attn_W_B"].reshape(D, N, D).transpose(2, 1, 0).reshape(D, N * D),
        "WCT": a["L0_attn_W_C"].reshape(D, N, D).transpose(2, 1, 0).reshape(D, N * D),
        "W1": a["L0_ffn_W1"],
        "b1": a["L0_ffn_b1"].reshape(E, FC, P).transpose(0, 2, 1),
        "W2": a["L0_ffn_W2"],
        "b2": a["L0_ffn_b2"],
        "Wr": a["L0_ffn_Wr"],
        "br": a["L0_ffn_br"],
    }
    arrays = {k: np.ascontiguousarray(v) for k, v in arrays.items()}
    nc = bacc.Bacc("TRN2", target_bir_lowering=False, num_devices=1)
    io = {k: nc.dram_tensor(f"in_{k}", v.shape, mybir.dt.from_np(v.dtype), kind="ExternalInput").ap()
          for k, v in arrays.items()}
    io["out"] = nc.dram_tensor("out", (B, L, D), F32, kind="ExternalOutput").ap()
    program(nc, io)
    r = run_bass_kernel_spmd(nc, [{f"in_{k}": v for k, v in arrays.items()}], core_ids=[0])
    return r.results[0]["out"]
```

```python
from contextlib import ExitStack

import concourse.bass as bass
import concourse.mybir as mybir
from concourse.alu_op_type import AluOpType as ALU

F32 = mybir.dt.float32
F16 = mybir.dt.float16
I32 = mybir.dt.int32
U32 = mybir.dt.uint32
ACT = mybir.ActivationFunctionType
AX = mybir.AxisListType

P = 128
B, L, D = 2, 2048, 256
T = B * L
N = 16
E = 8
F = 1024
KC = D // P
FC = F // P
NT = T // P
CH = 512
CT = CH // P
NCH = T // CH
RCH = L // CH
EPS = 1e-5
WSCALE = 64.0
BT = 256
BS = BT // P
NBLK = 2 * T // BT + E - 1
NSLOT = NBLK * BT
MAXB = T // BT
BIG = 3.0e38
TILES = KC * N
PIECE = 1024
NPIECE = 4


class Chain:

    def __init__(self, eng, sem):
        self.eng, self.sem, self.n = eng, sem, 0

    def run(self, ins):
        self.n += 1
        ins.then_inc(self.sem, 1)
        self.eng.wait_ge(self.sem, self.n)


def project_z(nc, keep, out, c, done):
    for hf in range(KC):
        k = 0
        for kc in range(KC):
            for a, b in ((0, 0), (0, 1), (1, 0)):
                k += 1
                ins = nc.tensor.matmul(out[hf][:], keep["Wd"][:, a, kc, hf * P:(hf + 1) * P],
                                       keep["xT"][:, bass.ds(c, 1), b, kc, :].squeeze(1),
                                       start=(k == 1), stop=(k == 3 * KC))
    ins.then_inc(done, 1)


def softplus_parts(nc, act, keep, src, z_ready, z_count, chain, chain_at, taken, ln_done):
    act.wait_ge(z_ready, z_count)
    for hf in range(KC):
        bias = keep["dbias"][:, hf:hf + 1]
        nc.scalar.activation(keep["zt"][:, hf], src[hf][:], ACT.Abs, scale=1.0 / WSCALE, bias=bias).then_inc(chain, 1)
        ins = nc.scalar.activation(keep["rel"][:, hf], src[hf][:], ACT.Relu, scale=1.0 / WSCALE, bias=bias)
        if taken is not None:
            ins.then_inc(taken, 1)
    act.wait_ge(chain, chain_at + KC)
    nc.scalar.activation(keep["zt"][:], keep["zt"][:], ACT.Exp, scale=-1.0).then_inc(chain, 1)
    act.wait_ge(chain, chain_at + (KC + 1))
    nc.scalar.activation(keep["zt"][:], keep["zt"][:], ACT.Ln, bias=1.0).then_inc(ln_done, 1)


def prologue(nc, io, keep, banks, ctx):
    def sb(name, shape, dt):
        return ctx.enter_context(nc.sbuf_tensor(name, shape, dt))

    def sem(name):
        return ctx.enter_context(nc.semaphore(name))

    GN = 2
    GW = GN * D
    NG = N // GN
    stB, stC = (keep["yall"][:, m:m + 2].rearrange("p a b c -> p (a b c)").rearrange(
        "p (r c m) -> p r c m", r=2, c=KC) for m in (0, 2))
    rows = keep["rows"]
    xall = keep["x"]
    xcur = sb("xcur", [P, 2, CT, D], F32)
    stWd = sb("stWd", [P, KC, D], F32)
    Wd = keep["Wd"]
    stWr = sb("stWr", [P, KC, E], F32)
    Wr = sb("Wr", [P, 2, KC, E], F16)
    brb = sb("brb", [P, E], F32)
    stats = sb("stats", [P, NT, 6], F32)
    mean = sb("mean", [P, NT], F32)
    rstd = sb("rstd", [P, NT], F32)
    std = sb("std", [P, NT], F32)
    var = sb("var", [P, NT], F32)
    ident, ident16 = keep["ident"], keep["ident16"]
    ones = sb("ones", [P, P], F16)
    tri = sb("tri", [P, P], F16)
    rev = sb("rev", [P, E], F32)
    thr = sb("thr", [P, MAXB], F32)
    blk = sb("blk", [P, NBLK], F32)
    one_r = sb("one_r", [P, NT * E], F32)
    zero = keep["yall"][:, NCH - 1, 0, 0:D]
    rel, zt, dcur = keep["rel"], keep["zt"], keep["dcur"]

    small_in = sem("small_in")
    b_in = [sem("b_in0"), sem("b_in1")]
    c_in = [sem("c_in0"), sem("c_in1")]
    XP = 4
    x_in = [sem(f"x_in{k}") for k in range(XP)]
    consts = sem("consts")
    zero_set = sem("zero_set")
    b_hi = sem("b_hi")
    b_lo = sem("b_lo")
    c_hi = sem("c_hi")
    c_lo = sem("c_lo")
    wd_hi = sem("wd_hi")
    wd_lo = sem("wd_lo")
    stat_chain = sem("stat_chain")
    act_chain = sem("act_chain")
    var_ready = sem("var_ready")
    std_ready = sem("std_ready")
    xn_ready = sem("xn_ready")
    row_hi = sem("row_hi")
    row_lo = sem("row_lo")
    c_scaled = sem("c_scaled")
    xt_ready = sem("xt_ready")
    xt_done = [[sem(f"xt_done{par}{kc}") for kc in range(KC)] for par in range(2)]
    gap_ready = sem("gap_ready")
    gap_exp = sem("gap_exp")
    cnt_ready = sem("cnt_ready")
    cnt_sum = sem("cnt_sum")
    sc_ready = sem("sc_ready")
    z_ready = sem("z_ready")
    z_chain = sem("z_chain")
    ln_ready = sem("ln_ready")
    delta_ready = sem("delta_ready")

    wb_v = io["WBT"].rearrange("(c p) m -> p c m", p=P)
    wc_v = io["WCT"].rearrange("(c p) m -> p c m", p=P)
    WB = keep["WB"][:].rearrange("p h c n d -> p h c (n d)")
    WC = keep["WC"][:].rearrange("p h c n d -> p h c (n d)")
    xT = keep["xT"]

    def router_sb(name):
        return sb(name, [P, NT, E], F32)

    sc, oh1, oh2, tmp = router_sb("sc"), router_sb("oh1"), router_sb("oh2"), router_sb("tmp")
    mx = sb("mx", [P, 2, NT], F32)
    top = sb("top", [P, NT], F32)
    M = sb("M", [P, E, NT], F32)
    cs = sb("cs", [P, E, NT], F32)
    rowc = sb("rowc", [P, E], F16)
    before = sb("before", [P, E], F32)
    nblk = sb("nblk", [P, E], F32)
    endb = sb("endb", [P, E], F32)
    off = sb("off", [P, E], F32)
    cmpb = sb("cmpb", [P, E, MAXB], F32)
    cmpe = sb("cmpe", [P, NBLK, E], F32)
    slotf = sb("slotf", [P, 2, NT], F32)
    ebf = sb("ebf", [P, NBLK], F32)

    def xt_at(part, kc, i, par, lo=0, n=CH):
        return xT[:, bass.ds(i * 2 + par, 1), part, kc, lo:lo + n].squeeze(1)

    def row_at(part, i, par):
        return rows[:, bass.ds(i * (2 * CT) + par * CT, CT), part, :]

    def turned_parts(par, kc):
        return banks[par * KC + kc][:].bitcast(F16).rearrange("p (b t) -> p b t", b=2)

    block = ctx.enter_context(nc.Block())

    @block.sync
    def _(sp):
        for k in range(XP):
            tiles = slice(k * NT // XP, (k + 1) * NT // XP)
            sp.dma_start(xall[:, tiles, :], io["x_tok"][:, tiles, :]).then_inc(x_in[k], 16)
        sp.dma_start(stWd[:], io["WdT"].rearrange("(c p) m -> p c m", p=P)).then_inc(small_in, 16)
        sp.dma_start(stWr[:], io["Wr"].rearrange("(c p) m -> p c m", p=P)).then_inc(small_in, 16)
        sp.dma_start(brb[:], io["br"].partition_broadcast(P)).then_inc(small_in, 16)
        sp.dma_start(keep["A"][:], io["A"].rearrange("(h p) n -> p h n", p=P)).then_inc(small_in, 16)
        sp.dma_start(keep["dbias"][:], io["dbias"]).then_inc(small_in, 16)
        with sp.Fori(0, NG // 2) as i:
            for par in range(2):
                at = i * (2 * GW) + par * GW
                sp.wait_ge(b_lo, i * 2 + (par + 1))
                sp.dma_start(stB[:, par], wb_v[:, :, bass.ds(at, GW)]).then_inc(b_in[par], 16)
                sp.wait_ge(c_lo, i * 2 + (par + 1))
                sp.dma_start(stC[:, par], wc_v[:, :, bass.ds(at, GW)]).then_inc(c_in[par], 16)
        sp.wait_ge(zero_set, 1)
        sp.dma_start(io["xs"].rearrange("(p r) d -> p r d", p=P),
                     zero.bitcast(F16).unsqueeze(1).broadcast_to([P, NSLOT // P, 2 * D])).then_inc(
                         keep["zeros_out"], 16)

    @block.gpsimd
    def _(pool):
        pool.sem_inc(c_lo, 2)
        pool.sem_inc(row_lo, 2)
        nc.gpsimd.memset(zero, 0.0).then_inc(zero_set, 1)
        nc.gpsimd.memset(ident[:], 0.0)
        nc.gpsimd.memset(tri[:], 1.0)
        nc.gpsimd.memset(ones[:], 1.0)
        nc.gpsimd.memset(one_r[:], 1.0).then_inc(consts, 1)
        pool.wait_ge(consts, 1)
        nc.gpsimd.affine_select(out=ident[:], in_=ident[:], compare_op=ALU.not_equal, fill=1.0, base=0,
                                pattern=[[-1, P]], channel_multiplier=1)
        nc.gpsimd.affine_select(out=tri[:], in_=tri[:], compare_op=ALU.is_gt, fill=0.0, base=0,
                                pattern=[[1, P]], channel_multiplier=-1)
        nc.gpsimd.iota(rev[:], pattern=[[-1, E]], base=E, channel_multiplier=0,
                       allow_small_or_imprecise_dtypes=True)
        nc.gpsimd.iota(thr[:], pattern=[[BT, MAXB]], base=0, channel_multiplier=0,
                       allow_small_or_imprecise_dtypes=True)
        nc.gpsimd.iota(blk[:], pattern=[[1, NBLK]], base=0, channel_multiplier=0,
                       allow_small_or_imprecise_dtypes=True).then_inc(consts, 1)
        pool.wait_ge(consts, 2)
        nc.gpsimd.tensor_copy(ident16[:], ident[:]).then_inc(consts, 1)
        def split_low(i):
            for par in range(2):
                pool.wait_ge(row_hi, i * 2 + (par + 1))
                nc.gpsimd.tensor_tensor(row_at(1, i, par), xcur[:, par], row_at(0, i, par),
                                        ALU.subtract).then_inc(row_lo, 1)

        def c_low(i):
            for par in range(2):
                pool.wait_ge(c_hi, i * 2 + (par + 1))
                at = i * (2 * GW) + par * GW
                nc.gpsimd.tensor_tensor(WC[:, 1, :, bass.ds(at, GW)], stC[:, par], WC[:, 0, :, bass.ds(at, GW)],
                                        ALU.subtract).then_inc(c_lo, 1)
        split_low(0)
        with pool.Fori(0, NG // 2 - 1) as i:
            c_low(i)
            split_low(i + 1)
        c_low(NG // 2 - 1)
        pool.wait_ge(ln_ready, 1)
        nc.gpsimd.tensor_tensor(dcur[:, 0], rel[:, 0], zt[:, 0], ALU.add).then_inc(delta_ready, 1)
        pool.wait_ge(delta_ready, 1)

    @block.scalar
    def _(act):
        act.wait_ge(small_in, 80)
        nc.scalar.activation(stWd[:], stWd[:], ACT.Copy, scale=WSCALE).then_inc(act_chain, 1)
        nc.scalar.activation(stWr[:], stWr[:], ACT.Copy, scale=WSCALE).then_inc(act_chain, 1)
        act.wait_ge(act_chain, 2)
        nc.scalar.activation(Wd[:, 0], stWd[:], ACT.Copy).then_inc(wd_hi, 1)
        nc.scalar.activation(Wr[:, 0], stWr[:], ACT.Copy).then_inc(wd_hi, 1)
        act.wait_ge(var_ready, 1)
        nc.scalar.activation(std[:], var[:], ACT.Sqrt).then_inc(std_ready, 1)

        def weight_group(i, par):
            at = i * (2 * GW) + par * GW
            act.wait_ge(b_in[par], i * 16 + 16)
            nc.scalar.activation(WB[:, 0, :, bass.ds(at, GW)], stB[:, par], ACT.Copy, scale=WSCALE).then_inc(b_hi, 1)
            act.wait_ge(c_in[par], i * 16 + 16)
            nc.scalar.activation(stC[:, par], stC[:, par], ACT.Copy, scale=WSCALE).then_inc(c_scaled, 1)
            act.wait_ge(c_scaled, i * 2 + (par + 1))
            nc.scalar.activation(WC[:, 0, :, bass.ds(at, GW)], stC[:, par], ACT.Copy).then_inc(c_hi, 1)

        def high_rows(i):
            for par in range(2):
                act.wait_ge(xn_ready, i * 2 + (par + 1))
                nc.scalar.activation(row_at(0, i, par), xcur[:, par], ACT.Copy).then_inc(row_hi, 1)

        def weights_and_copy(i, ahead):
            for par in range(2):
                weight_group(i, par)
            if ahead:
                high_rows(i + 1)
            act.wait_ge(xt_ready, i * (2 * KC) + 1)
            nc.scalar.activation(xt_at(slice(0, 2), 0, i, 0), turned_parts(0, 0), ACT.Copy).then_inc(xt_done[0][0], 1)

        act.sem_inc(xt_done[0][0], 1)
        high_rows(0)
        with act.Fori(0, NCH // 2 - 1) as i:
            weights_and_copy(i, True)
        weights_and_copy(NCH // 2 - 1, False)
        softplus_parts(nc, act, keep, banks[4:6], z_ready, 1, z_chain, 0, None, ln_ready)
        act.wait_ge(gap_ready, 1)
        nc.scalar.activation(keep["w"][:, 1, :], keep["w"][:, 0, :], ACT.Exp).then_inc(gap_exp, 1)

    @block.vector
    def _(dve):
        v = nc.vector
        dve.sem_inc(b_lo, 2)
        for par, kc in ((0, 1), (1, 0), (1, 1)):
            dve.sem_inc(xt_done[par][kc], 1)
        for k in range(XP):
            dve.wait_ge(x_in[k], 16)
            with dve.Fori(k * NT // XP // 4, (k + 1) * NT // XP // 4) as i:
                for q in range(4):
                    one = bass.ds(i * 4 + q, 1)
                    v.bn_stats(stats[:, one, :].rearrange("p a b -> p (a b)"),
                               xall[:, one, :].rearrange("p a b -> p (a b)")).then_inc(stat_chain, 1)
        ch = Chain(dve, stat_chain)
        ch.n = NT
        dve.wait_ge(stat_chain, ch.n)
        m_e, q_e, m_o, q_o = stats[:, :, 1], stats[:, :, 2], stats[:, :, 4], stats[:, :, 5]
        ch.run(v.tensor_tensor(mean[:], m_e, m_o, ALU.add))
        ch.run(v.tensor_scalar(mean[:], mean[:], 0.5, None, ALU.mult))
        ch.run(v.tensor_tensor(std[:], m_e, m_o, ALU.subtract))
        ch.run(v.scalar_tensor_tensor(std[:], std[:], 0.25, std[:], ALU.mult, ALU.mult))
        ch.run(v.tensor_tensor(var[:], q_e, q_o, ALU.add))
        ch.run(v.scalar_tensor_tensor(var[:], var[:], 1.0 / D, std[:], ALU.mult, ALU.add))
        ch.run(v.tensor_scalar(var[:], var[:], EPS, None, ALU.add))
        dve.sem_inc(var_ready, 1)
        dve.wait_ge(std_ready, 1)
        ch.run(v.reciprocal(rstd[:], std[:]))
        ch.run(v.tensor_tensor(std[:], rstd[:], rstd[:], ALU.mult))
        ch.run(v.tensor_tensor(std[:], std[:], var[:], ALU.mult))
        ch.run(v.tensor_scalar(std[:], std[:], -0.5, 1.5, ALU.mult, ALU.add))
        ch.run(v.tensor_tensor(rstd[:], rstd[:], std[:], ALU.mult))
        dve.wait_ge(wd_hi, 2)
        v.reciprocal(keep["rA"][:], keep["A"][:])
        v.tensor_tensor(Wd[:, 1], stWd[:], Wd[:, 0], ALU.subtract).then_inc(wd_lo, 1)
        v.tensor_tensor(Wr[:, 1], stWr[:], Wr[:, 0], ALU.subtract).then_inc(wd_lo, 1)
        def normalise(i):
            for par in range(2):
                dve.wait_ge(row_lo, i * 2 + (par + 1))
                for q in range(CT):
                    t = i * (2 * CT) + (par * CT + q)
                    ins = v.tensor_scalar(xcur[:, par, q, :], xall[:, bass.ds(t, 1), :].rearrange("p a b -> p (a b)"),
                                          mean[:, bass.ds(t, 1)], rstd[:, bass.ds(t, 1)],
                                          ALU.subtract, ALU.mult)
                ins.then_inc(xn_ready, 1)

        def weights_and_copy(i, ahead):
            for par in range(2):
                at = i * (2 * GW) + par * GW
                dve.wait_ge(b_hi, i * 2 + (par + 1))
                v.scalar_tensor_tensor(WB[:, 1, :, bass.ds(at, GW)], stB[:, par], WSCALE, WB[:, 0, :, bass.ds(at, GW)],
                                       ALU.mult, ALU.subtract).then_inc(b_lo, 1)
            if ahead:
                normalise(i + 1)
            for par, kc in ((0, 1), (1, 0), (1, 1)):
                dve.wait_ge(xt_ready, i * (2 * KC) + (par * KC + kc + 1))
                v.tensor_scalar(xt_at(slice(0, 2), kc, i, par), turned_parts(par, kc), 1.0, None,
                                ALU.mult).then_inc(xt_done[par][kc], 1)

        normalise(0)
        with dve.Fori(0, NCH // 2 - 1) as i:
            weights_and_copy(i, True)
        weights_and_copy(NCH // 2 - 1, False)

        dve.wait_ge(sc_ready, NCH)
        dve.wait_ge(consts, 2)

        def per_token(ap):
            return ap.unsqueeze(2).broadcast_to([P, NT, E])

        def per_expert(ap):
            return ap.unsqueeze(1).broadcast_to([P, NT, E])

        sc_ps = banks[6][:, 0:NT * E].rearrange("p (i e) -> p i e", e=E)
        ch.run(v.scalar_tensor_tensor(sc[:], sc_ps, 1.0 / WSCALE, per_expert(brb[:]), ALU.mult, ALU.add))
        for k, oh in ((0, oh1), (1, oh2)):
            ch.run(v.tensor_reduce(mx[:, k, :], sc[:], AX.X, ALU.max))
            ch.run(v.tensor_tensor(tmp[:], sc[:], per_token(mx[:, k, :]), ALU.is_equal))
            ch.run(v.tensor_tensor(tmp[:], tmp[:], per_expert(rev[:]), ALU.mult))
            ch.run(v.tensor_reduce(top[:], tmp[:], AX.X, ALU.max))
            ch.run(v.tensor_tensor(oh[:], per_expert(rev[:]), per_token(top[:]), ALU.is_equal))
            if k == 0:
                ch.run(v.scalar_tensor_tensor(sc[:], oh[:], -BIG, sc[:], ALU.mult, ALU.add))
        ch.run(v.tensor_tensor(keep["w"][:, 0, :], mx[:, 1, :], mx[:, 0, :], ALU.subtract))
        dve.sem_inc(gap_ready, 1)
        ch.run(v.tensor_tensor(M[:].rearrange("p e i -> p i e"), oh1[:], oh2[:], ALU.add))
        ch.run(v.tensor_tensor_scan(cs[:].rearrange("p e i -> p (e i)"), one_r[:], M[:].rearrange("p e i -> p (e i)"),
                                    0.0, ALU.mult, ALU.add))
        last = cs[:, :, NT - 1]
        ch.run(v.memset(before[:, 0:1], 0.0))
        ch.run(v.tensor_copy(before[:, 1:E], cs[:, 0:E - 1, NT - 1]))
        ch.run(v.tensor_tensor(rowc[:], last, before[:], ALU.subtract))
        dve.sem_inc(cnt_ready, 1)
        ch.run(v.tensor_tensor(cs[:], cs[:], M[:], ALU.subtract))
        dve.wait_ge(cnt_sum, 1)
        earlier, total = banks[7][:, 0:E], banks[7][:, E:2 * E]
        ch.run(v.tensor_tensor(cmpb[:], total.unsqueeze(2).broadcast_to([P, E, MAXB]),
                               thr[:].unsqueeze(1).broadcast_to([P, E, MAXB]), ALU.is_gt))
        ch.run(v.tensor_reduce(nblk[:], cmpb[:], AX.X, ALU.add))
        ch.run(v.tensor_tensor_scan(endb[:], one_r[:, 0:E], nblk[:], 0.0, ALU.mult, ALU.add))
        ch.run(v.tensor_tensor(off[:], endb[:], nblk[:], ALU.subtract))
        ch.run(v.scalar_tensor_tensor(off[:], off[:], float(BT), earlier, ALU.mult, ALU.add))
        ch.run(v.tensor_tensor(off[:], off[:], before[:], ALU.subtract))
        ch.run(v.tensor_tensor(cs[:], cs[:], off[:].unsqueeze(2).broadcast_to([P, E, NT]), ALU.add))
        for k, oh in ((0, oh1), (1, oh2)):
            ch.run(v.tensor_tensor(tmp[:], oh[:], cs[:].rearrange("p e i -> p i e"), ALU.mult))
            ch.run(v.tensor_reduce(slotf[:, k, :], tmp[:], AX.X, ALU.add))
        ch.run(v.tensor_copy(keep["slot"][:], slotf[:]))
        ch.run(v.tensor_tensor(cmpe[:], endb[:].unsqueeze(1).broadcast_to([P, NBLK, E]),
                               blk[:].unsqueeze(2).broadcast_to([P, NBLK, E]), ALU.is_le))
        ch.run(v.tensor_reduce(ebf[:], cmpe[:], AX.X, ALU.add))
        ch.run(v.tensor_scalar(keep["eblk"][:], ebf[:], float(E - 1), None, ALU.min))
        dve.wait_ge(gap_exp, 1)
        ch.run(v.tensor_scalar(top[:], keep["w"][:, 1, :], 1.0, None, ALU.add))
        ch.run(v.reciprocal(keep["w"][:, 0, :], top[:]))
        ch.run(v.tensor_tensor(keep["w"][:, 1, :], keep["w"][:, 1, :], keep["w"][:, 0, :], ALU.mult))

    @block.tensor
    def _(pe):
        mm = nc.tensor.matmul
        pe.wait_ge(consts, 3)
        pe.wait_ge(wd_lo, 2)
        with pe.Fori(0, NCH // 2) as i:
            for par in range(2):
                pe.wait_ge(row_lo, i * 2 + (par + 1 + 2))
                for done in xt_done[par]:
                    pe.wait_ge(done, i + 1)
                for kc in range(KC):
                    for b in range(2):
                        for q in range(CT):
                            t = bass.ds(i * (2 * CT) + (par * CT + q), 1)
                            ins = nc.tensor.transpose(turned_parts(par, kc)[:, b, q * P:(q + 1) * P],
                                                      rows[:, t, b, kc * P:(kc + 1) * P].squeeze(1), ident16[:])
                    ins.then_inc(xt_ready, 1)
            for par in range(2):
                for done in xt_done[par]:
                    pe.wait_ge(done, i + 2)
                for q in range(CT):
                    n = 0
                    for kc in range(KC):
                        for a, b in ((0, 0), (0, 1), (1, 0), (1, 1)):
                            n += 1
                            ins = mm(banks[6][:, bass.ds(i * (2 * CT * E) + (par * CT + q) * E, E)],
                                     xt_at(a, kc, i, par, q * P, P), Wr[:, b, kc, :],
                                     start=(n == 1), stop=(n == 4 * KC))
                ins.then_inc(sc_ready, 1)
        project_z(nc, keep, banks[4:6], 0, z_ready)
        pe.wait_ge(cnt_ready, 1)
        mm(banks[7][:, 0:E], tri[:], rowc[:], start=True, stop=True)
        mm(banks[7][:, E:2 * E], ones[:], rowc[:], start=True, stop=True).then_inc(cnt_sum, 1)


def expert_of(eng, keep, b):
    return eng.value_load(keep["eblk"][0:1, bass.ds(b, 1)], min_val=0, max_val=E - 1)


def load_w1(sp, io, keep, ex, par):
    sp.dma_start(keep["w1"][:, par], io["wsplit"][bass.ds(ex, 1), :, 0:KC].rearrange("a p c h f -> p (a c) h f"))\
        .then_inc(keep["w1_in"][par], 16)
    sp.dma_start(keep["b1"][:, par], io["b1"][bass.ds(ex, 1)].rearrange("a p c -> p (a c)"))\
        .then_inc(keep["w1_in"][par], 16)


def load_slots(sp, io, keep, b, par):
    xs_v = io["xs"].rearrange("(b s p) d -> p b s d", s=BS, p=P)
    sp.dma_start(keep["xb"][:, par], xs_v[:, bass.ds(b, 1)].rearrange("p b s d -> p (b s) d"))\
        .then_inc(keep["xb_in"][par], 16)


def scan_phase(nc, io, keep, banks, ctx, row):
    split_weights, combine = row == 0, row == 1

    def sb(name, shape, dt):
        return ctx.enter_context(nc.sbuf_tensor(f"{name}_{row}", shape, dt))

    def sem(name):
        return ctx.enter_context(nc.semaphore(f"{name}_{row}"))

    AR = 4
    aexp = sb("aexp", [P, AR, CH], F32)
    ub = sb("ub", [P, 2, CH], F32)
    uxb = sb("uxb", [P, 2, CH], F32)
    hb = sb("hb", [P, AR, CH], F32)
    hcb = sb("hcb", [P, 2, CH], F32)
    x32 = sb("x32", [P, KC, CH], F32)
    state = sb("state", [P, TILES], F32)
    Bps, Cps, Yps, Ops = banks[0:2], banks[2:4], banks[4:6], banks[6:8]
    xT, WB, WC, A = keep["xT"], keep["WB"], keep["WC"], keep["A"]
    rel, zt, dcur, yall = keep["rel"], keep["zt"], keep["dcur"], keep["yall"]

    a_ready = sem("a_ready")
    B_ready = sem("B_ready")
    C_ready = sem("C_ready")
    u_done = sem("u_done")
    ux_done = sem("ux_done")
    h_done = sem("h_done")
    hc_done = sem("hc_done")
    acc_done = sem("acc_done")
    state_saved = sem("state_saved")
    x32_done = [sem("x32_done0"), sem("x32_done1")]
    z_ready = sem("z_ready")
    z_taken = sem("z_taken")
    z_chain = sem("z_chain")
    ln_done = sem("ln_done")
    delta_done = sem("delta_done")
    U_CR, UX_CR, H_CR, HC_CR, ACC_CR, ST_CR, D_CR = 2, 1, AR, 2, 1, AR, 1
    AHEAD = AR - 1
    ACCS = TILES - KC
    Z_AT, Z_LOG, D_NEXT, D_HERE = 3, 6, 20, 2

    if split_weights:
        stage = yall[:, RCH:NCH].rearrange("p a b c -> p (a b c)")
        wst = stage[:, 0:2 * PIECE].rearrange("p (r f) -> p r f", r=2)
        whl = stage[:, 2 * PIECE:4 * PIECE].bitcast(F16).rearrange("p (r h f) -> p r h f", r=2, h=2)
        piece_in = [sem("piece_in0"), sem("piece_in1")]
        piece_out = [sem("piece_out0"), sem("piece_out1")]
        p_scaled = sem("p_scaled")
        p_hi = sem("p_hi")
        p_lo = sem("p_lo")
    if combine:
        gat = xT[:, 0:RCH].rearrange("p a b c d -> p (a b c d)").bitcast(F32).rearrange(
            "p (g q k d) -> p g q k d", g=2, q=CT, k=2)
        ycur = sb("ycur", [P, 2, KC, CH], F32)
        xres = sb("xres", [P, 2, CT, D], F32)
        ob = sb("ob", [P, 2, CT, D], F32)
        sidx = sb("sidx", [P, 2, 2, CT], U32)
        ycur_done = sem("ycur_done")
        idx_done = sem("idx_done")
        turned = sem("turned")
        gathered = [sem("gathered0"), sem("gathered1")]
        xres_in = [sem("xres_in0"), sem("xres_in1")]
        weighted = [sem("weighted0"), sem("weighted1")]
        experts_added = [sem("experts_added0"), sem("experts_added1")]
        x_added = [sem("x_added0"), sem("x_added1")]
        o_ready = sem("o_ready")
        out_sent = [sem("out_sent0"), sem("out_sent1")]
    WEIGH_AT, ADD_AT, TURN_AT, CLOSE_AT = (10, 19), (15, 24), (8, 22), (19, 28)

    def tile(s):
        return s // N, s % N

    def chunk(t, c):
        return t[:, bass.ds(c + row * RCH, 1)].squeeze(1)

    def group_chunk(c, g, last):
        return NCH - 1 if last and g == 0 else c + 3 * g

    def group_at(c, g, last):
        return c * 2 + (1 - g if last else g)

    def group_tiles(c, g, last):
        return bass.ds(group_chunk(c, g, last) * CT, CT)

    def chunks(eng, body):
        with eng.Fori(0, RCH - 1) as c:
            body(c, False, False)
        body(RCH - 1, combine, True)

    PIECES = E * NPIECE // RCH
    EPC = E // RCH
    STRIDE = 3

    def store_piece(sp, c, k):
        ex = c * EPC + k // NPIECE
        sp.wait_ge(p_lo, c * PIECES + (k + 1 + 2))
        sp.dma_start(io["wsplit"][bass.ds(ex, 1), :, k % NPIECE, :, :].rearrange("a p h f -> p (a h) f"),
                     whl[:, k % 2]).then_inc(piece_out[k % 2], 16)

    block = ctx.enter_context(nc.Block())

    @block.sync
    def _(sp):
        if split_weights:
            with sp.Fori(0, RCH) as c:
                for k in range(PIECES):
                    par = k % 2
                    ex = c * EPC + k // NPIECE
                    pc = k % NPIECE
                    sp.wait_ge(p_lo, c * PIECES + (k + 1))
                    if pc < KC:
                        src = io["W1"][bass.ds(ex, 1), pc * P:(pc + 1) * P, :].rearrange("a p f -> p (a f)")
                        sp.dma_start(wst[:, par, :], src).then_inc(piece_in[par], 16)
                    else:
                        fc = (pc - KC) * (FC // 2)
                        src = io["W2"][bass.ds(ex, 1), fc * P:(fc + FC // 2) * P, :]\
                            .rearrange("a (c p) d -> p (a c) d", p=P)
                        sp.dma_start(wst[:, par, :].rearrange("p (c d) -> p c d", d=D), src).then_inc(piece_in[par], 16)
                    if k >= 1:
                        store_piece(sp, c, k - 1)
                store_piece(sp, c, PIECES - 1)
            for par in range(2):
                sp.wait_ge(piece_out[par], (RCH * PIECES // 2 + 1) * 16)
            sp.wait_ge(B_ready, (RCH - 1) * TILES + 1)
            sp.wait_ge(C_ready, (RCH - 1) * TILES + 1)
            for hf in range(2):
                sp.wait_ge(x32_done[hf], RCH - 1)
            load_w1(sp, io, keep, expert_of(sp, keep, 0), 0)
            sp.wait_ge(keep["scattered"], 2 * NT * 16)
            for par in range(2):
                load_slots(sp, io, keep, par, par)

        def body(c, last, final):
            order = (1, 0) if last else (0, 1)
            for g in order:
                sp.wait_ge(o_ready, c * 2 + (g + 1))
                sp.dma_start(xres[:, g], io["x_tok"][:, group_tiles(c, g, last), :]).then_inc(xres_in[g], 16)
            for g in order:
                sp.wait_ge(o_ready, group_at(c, g, last) + 3)
                sp.dma_start(io["out_tok"][:, group_tiles(c, g, last), :], ob[:, g]).then_inc(out_sent[g], 16)

        if combine:
            chunks(sp, body)
            for g in range(2):
                sp.wait_ge(out_sent[g], (RCH + 1) * 16)

    @block.scalar
    def _(act):
        act.sem_inc(state_saved, ST_CR)
        if split_weights:
            act.wait_ge(keep["zeros_out"], 16)
        act.sem_inc(z_taken, KC)

        def save_state(c, s):
            act.wait_ge(h_done, c * TILES + (s + 1 + H_CR))
            nc.scalar.activation(state[:, s:s + 1], hb[:, s % AR, CH - 1:CH], ACT.Copy).then_inc(state_saved, 1)

        def exp_tile(c, s):
            hf, n = tile(s % TILES)
            if n == 0:
                act.wait_ge(delta_done, c * 2 + (s // N + 1))
            act.wait_ge(h_done, c * TILES + (s + 1))
            nc.scalar.activation(aexp[:, s % AR], dcur[:, hf, :], ACT.Exp,
                                 scale=A[:, hf, n:n + 1]).then_inc(a_ready, 1)

        def body(c, last, final):
            for s in range(TILES):
                if not (final and s + AHEAD >= TILES):
                    exp_tile(c, s + AHEAD)
                save_state(c, s)
                if s == Z_LOG and not last:
                    act.wait_ge(delta_done, c * 2 + 2)
                    softplus_parts(nc, act, keep, Ops, z_ready, c + 1, z_chain, c * (KC + 1), z_taken, ln_done)
                if split_weights and s % STRIDE == 1 and s // STRIDE < PIECES:
                    k = s // STRIDE
                    par = k % 2
                    act.wait_ge(piece_in[par], (c * (PIECES // 2) + (k // 2 + 1)) * 16)
                    nc.scalar.activation(wst[:, par, :], wst[:, par, :], ACT.Copy, scale=WSCALE).then_inc(p_scaled, 1)
                    act.wait_ge(piece_out[par], (c * (PIECES // 2) + (k // 2 + 1)) * 16)
                    act.wait_ge(p_scaled, c * PIECES + (k + 1))
                    nc.scalar.activation(whl[:, par, 0, :], wst[:, par, :], ACT.Copy).then_inc(p_hi, 1)
                if combine and s in (5, 19) and not (last and s == 5):
                    take_y(c, s // 19, last)
                for g in range(2) if combine else ():
                    if WEIGH_AT[g] <= s < WEIGH_AT[g] + CT:
                        weigh(c, g, s - WEIGH_AT[g], last)
            if last:
                take_y(c, 0, last)

        def weigh(c, g, q, last):
            tok = bass.ds(group_chunk(c, g, last) * CT + q, 1)
            if q == 0:
                act.wait_ge(gathered[g], c * (2 * CT * 16) + 2 * CT * 16)
            for k in range(2):
                ins = nc.scalar.activation(gat[:, g, q, k], gat[:, g, q, k], ACT.Copy, scale=keep["w"][:, k, tok])
            if q == CT - 1:
                ins.then_inc(weighted[g], 1)

        def take_y(c, g, last):
            act.wait_ge(acc_done, (c + (1 if last and g == 0 else 0)) * ACCS + 1)
            act.wait_ge(turned, group_at(c, g, last) + 1)
            nc.scalar.activation(ycur[:, g], yall[:, bass.ds(group_chunk(c, g, last), 1)].squeeze(1), ACT.Copy,
                                 scale=1.0 / (WSCALE * WSCALE)).then_inc(ycur_done, 1)

        for s in range(AHEAD):
            exp_tile(0, s)
        chunks(act, body)

    @block.gpsimd
    def _(pool):
        pool.sem_inc(ux_done, UX_CR)
        pool.sem_inc(delta_done, D_CR)
        if split_weights:
            pool.sem_inc(p_lo, 2)
            pool.sem_inc(piece_out[0], 16)
            pool.sem_inc(piece_out[1], 16)
            pool.wait_ge(keep["zeros_out"], 16)
        if combine:
            pool.sem_inc(out_sent[0], 16)
            pool.sem_inc(out_sent[1], 16)

        def restore_x(c, hf, products):
            pool.wait_ge(ux_done, products + 1)
            nc.gpsimd.tensor_tensor(x32[:, hf], chunk(xT, c)[:, 0, hf], chunk(xT, c)[:, 1, hf],
                                    ALU.add).then_inc(x32_done[hf], 1)

        def body(c, last, final, scatter=()):
            if combine:
                for g in range(2):
                    ins = nc.gpsimd.tensor_copy(sidx[:, g], keep["slot"][:, :, group_tiles(c, g, last)])
                ins.then_inc(idx_done, 1)
                pool.wait_ge(idx_done, c + 1)
            for s in range(TILES):
                hf, n = tile(s)
                pool.wait_ge(u_done, c * TILES + (s + 1 + U_CR))
                pool.wait_ge(h_done, c * TILES + (s + AR - 1))
                if n == 0:
                    pool.wait_ge(x32_done[hf], c + 1)
                nc.gpsimd.tensor_tensor(uxb[:, s % 2], ub[:, s % 2], x32[:, hf], ALU.mult).then_inc(ux_done, 1)
                if s == 5:
                    restore_x(c, 1, c * TILES)
                if s == 23 and not final:
                    restore_x(c + 1, 0, c * TILES + N)
                if s == D_HERE:
                    pool.wait_ge(a_ready, c * TILES + 1)
                    nc.gpsimd.tensor_tensor(dcur[:, 1], rel[:, 1], zt[:, 1], ALU.add).then_inc(delta_done, 1)
                if s == D_NEXT and not last:
                    pool.wait_ge(a_ready, c * TILES + N)
                    pool.wait_ge(ln_done, c + 1)
                    nc.gpsimd.tensor_tensor(dcur[:, 0], rel[:, 0], zt[:, 0], ALU.add).then_inc(delta_done, 1)
                if split_weights and s % STRIDE == 2 and 1 <= s // STRIDE <= PIECES:
                    k = s // STRIDE - 1
                    par = k % 2
                    pool.wait_ge(p_hi, c * PIECES + (k + 1))
                    nc.gpsimd.tensor_tensor(whl[:, par, 1, :], wst[:, par, :], whl[:, par, 0, :],
                                            ALU.subtract).then_inc(p_lo, 1)
                nth = s - (s + 1) // STRIDE
                for i, k in scatter[nth:nth + 1] if s % STRIDE != 2 else ():
                    nc.gpsimd.indirect_dma_start(
                        out=io["xs"], out_offset=bass.IndirectOffsetOnAxis(keep["slot"][:, k, i:i + 1], 0),
                        in_=keep["rows"][:, i].rearrange("p a d -> p (a d)"),
                        in_offset=None).then_inc(keep["scattered"], 16)
                for g in range(2) if combine else ():
                    if s == ADD_AT[g]:
                        pool.wait_ge(weighted[g], c + 1)
                        pool.wait_ge(out_sent[g], c * 16 + 16)
                        nc.gpsimd.tensor_tensor(ob[:, g], gat[:, g, :, 0], gat[:, g, :, 1],
                                                ALU.add).then_inc(experts_added[g], 1)
                    if s == ADD_AT[g] + 2:
                        pool.wait_ge(experts_added[g], c + 1)
                        pool.wait_ge(xres_in[g], c * 16 + 16)
                        nc.gpsimd.tensor_tensor(ob[:, g], ob[:, g], xres[:, g], ALU.add).then_inc(x_added[g], 1)
                if combine and s == 0:
                    for k in range(2):
                        pool.wait_ge(keep["y_out"][k], (NBLK // 2 + 2 - k) * 16)
                if combine and s < 4 * CT:
                    g, q, k = s // (2 * CT), s % (2 * CT) // 2, s % 2
                    nc.gpsimd.indirect_dma_start(
                        out=gat[:, g, q, k, :], out_offset=None, in_=io["ys"],
                        in_offset=bass.IndirectOffsetOnAxis(sidx[:, g, k, q:q + 1], 0)).then_inc(gathered[g], 16)

        restore_x(0, 0, 0)
        if split_weights:
            todo = [(i, k) for i in range(NT) for k in range(2)]
            for c in range(RCH):
                body(c, False, c == RCH - 1, todo[c * len(todo) // RCH:(c + 1) * len(todo) // RCH])
            pool.wait_ge(keep["scattered"], len(todo) * 16)
        else:
            chunks(pool, body)

    @block.vector
    def _(dve):
        v = nc.vector
        dve.sem_inc(u_done, U_CR)
        dve.sem_inc(h_done, H_CR)
        dve.sem_inc(hc_done, HC_CR)
        dve.sem_inc(acc_done, ACC_CR)
        if combine:
            dve.sem_inc(o_ready, 2)
        v.memset(state[:], 0.0)

        def u_op(c, s):
            dve.wait_ge(a_ready, c * TILES + (s + 1))
            dve.wait_ge(B_ready, c * TILES + (s + 1))
            v.scalar_tensor_tensor(ub[:, s % 2], aexp[:, s % AR], -1.0, Bps[s % 2][:], ALU.add,
                                   ALU.mult).then_inc(u_done, 1)

        def scan_op(c, s):
            dve.wait_ge(ux_done, c * TILES + (s + 1 + UX_CR))
            dve.wait_ge(state_saved, c * TILES + (s + 1))
            v.tensor_tensor_scan(hb[:, s % AR], aexp[:, s % AR], uxb[:, s % 2], state[:, s:s + 1],
                                 ALU.mult, ALU.add).then_inc(h_done, 1)

        def hc_op(c, s):
            hf, n = tile(s)
            dve.wait_ge(C_ready, c * TILES + (s + 1))
            dve.wait_ge(h_done, c * TILES + (s + 1 + H_CR))
            dst = Yps[hf][:] if n == 0 else hcb[:, s % 2]
            v.scalar_tensor_tensor(dst, hb[:, s % AR], keep["rA"][:, hf, n:n + 1], Cps[s % 2][:], ALU.mult,
                                   ALU.mult).then_inc(hc_done, 1)

        def acc_op(c, s):
            hf, n = tile(s)
            if n == 0:
                return
            dve.wait_ge(hc_done, c * TILES + (s + 1 + HC_CR))
            dve.wait_ge(acc_done, c * ACCS + (hf * (N - 1) + n - 1 + ACC_CR))
            dst = chunk(yall, c)[:, hf] if n == N - 1 else Yps[hf][:]
            v.tensor_tensor(dst, Yps[hf][:], hcb[:, s % 2], ALU.add).then_inc(acc_done, 1)

        def close_op(c, g, half, last):
            if half == 0:
                dve.wait_ge(x_added[g], c + 1)
                dve.wait_ge(turned, group_at(c, g, last) + 3)
            ins = v.tensor_tensor(ob[:, g, half * 2:half * 2 + 2], ob[:, g, half * 2:half * 2 + 2],
                                  Ops[half][:].rearrange("p (q d) -> p q d", q=2), ALU.add)
            if half == 1:
                ins.then_inc(o_ready, 1)

        def body(c, last, final):
            for s in range(1, TILES + 1):
                if not (final and s == TILES):
                    u_op(c, s)
                scan_op(c, s - 1)
                if s >= 2:
                    acc_op(c, s - 2)
                hc_op(c, s - 1)
                for g in range(2) if combine else ():
                    if CLOSE_AT[g] <= s < CLOSE_AT[g] + 2 and not (last and g == 0):
                        close_op(c, g, s - CLOSE_AT[g], last)
            acc_op(c, TILES - 1)
            if last:
                for half in range(2):
                    close_op(c, 0, half, last)

        u_op(0, 0)
        chunks(dve, body)

    @block.tensor
    def _(pe):
        mm = nc.tensor.matmul
        if combine:
            pe.sem_inc(turned, 2)

        def project(bank, W, c, s, done):
            hf, n = tile(s)
            k = 0
            for kc in range(KC):
                for a, b in ((0, 0), (0, 1), (1, 0)):
                    k += 1
                    ins = mm(bank[:], W[:, a, kc, n, hf * P:(hf + 1) * P], chunk(xT, c)[:, b, kc, :],
                             start=(k == 1), stop=(k == 3 * KC))
            ins.then_inc(done, 1)

        def project_c(c, s):
            pe.wait_ge(hc_done, c * TILES + (s + 1))
            project(Cps[s % 2], WC, c, s, C_ready)

        def turn(c, g, last):
            pe.wait_ge(ycur_done, group_at(c, g, last) + 1)
            pe.wait_ge(o_ready, group_at(c, g, last) + 2)
            pe.wait_ge(z_taken, (c + (0 if last else 1)) * KC + KC)
            for q in range(CT):
                for hf in range(KC):
                    col = q % 2 * D + hf * P
                    ins = nc.tensor.transpose(Ops[q // 2][:, col:col + P], ycur[:, g, hf, q * P:(q + 1) * P],
                                              keep["ident"][:])
            ins.then_inc(turned, 1)

        def project_b(c, s):
            pe.wait_ge(u_done, c * TILES + (s + 1))
            project(Bps[s % 2], WB, c + s // TILES, s % TILES, B_ready)

        def body(c, last, final):
            for s in range(1, TILES + 1):
                if not (final and s == TILES):
                    project_b(c, s)
                project_c(c, s - 1)
                if s == Z_AT and not last:
                    if combine:
                        pe.wait_ge(o_ready, c * 2 + 2)
                    pe.wait_ge(z_taken, c * KC + KC)
                    project_z(nc, keep, Ops, c + (row * RCH + 1), z_ready)
                if combine and s == TURN_AT[0] and not last:
                    turn(c, 0, last)
                if combine and s == TURN_AT[1]:
                    turn(c, 1, last)
            if last:
                turn(c, 0, last)

        project_b(0, 0)
        chunks(pe, body)


def expert_phase(nc, io, keep, banks, ctx):
    def sb(name, shape, dt):
        return ctx.enter_context(nc.sbuf_tensor(name, shape, dt))

    def sem(name):
        return ctx.enter_context(nc.semaphore(name))

    w1, b1, xb = keep["w1"], keep["b1"], keep["xb"]
    hs = sb("hs", [P, 2, 2, FC, BT], F16)
    w2 = sb("w2", [P, 2, 2, 2, FC // 2, D], F16)
    b2 = sb("b2", [P, 2, D], F32)
    xbt = sb("xbt", [P, 2, 2, KC, BT], F16)
    h32 = sb("h32", [P, FC, BT], F32)
    yo = sb("yo", [P, 2, BS, D], F32)
    Hps, Tps, Yps = banks[0:4], banks[4:6], banks[6:8]

    w1_in, xb_in = keep["w1_in"], keep["xb_in"]
    w2_in = [sem("w2_in0"), sem("w2_in1")]
    y_out = keep["y_out"]
    T_done = sem("T_done")
    H_done = sem("H_done")
    Y_done = sem("Y_done")
    xbt_done = sem("xbt_done")
    gelu_done = sem("gelu_done")
    hhi_done = sem("hhi_done")
    hlo_done = sem("hlo_done")
    y_taken = sem("y_taken")
    PAIRS = FC // 2
    ys_v = io["ys"].rearrange("(b s p) d -> p b s d", s=BS, p=P)

    block = ctx.enter_context(nc.Block())


    @block.sync
    def _(sp):
        def slots(b, par):
            sp.wait_ge(T_done, b + 1)
            load_slots(sp, io, keep, b, par)

        def weights(b, par):
            ex = expert_of(sp, keep, b)
            sp.wait_ge(H_done, b * PAIRS + PAIRS)
            sp.wait_ge(gelu_done, b * FC + FC)
            load_w1(sp, io, keep, ex, par)

        def store(b, par):
            sp.wait_ge(y_taken, b + (1 + 2))
            sp.dma_start(ys_v[:, bass.ds(b, 1)].rearrange("p b s d -> p (b s) d"), yo[:, par]).then_inc(y_out[par], 16)

        sp.sem_inc(y_out[0], 16)
        sp.sem_inc(y_out[1], 16)
        weights(1, 1)
        slots(2, 0)
        weights(2, 0)
        slots(3, 1)
        with sp.Fori(0, (NBLK - 5) // 2) as i:
            for m in range(2):
                weights(i * 2 + (m + 3), (m + 1) % 2)
                slots(i * 2 + (m + 4), m)
                store(i * 2 + m, m)
        weights(NBLK - 2, 1)
        slots(NBLK - 1, 0)
        store(NBLK - 5, 0)
        weights(NBLK - 1, 0)
        for b in range(NBLK - 4, NBLK):
            store(b, b % 2)

    @block.gpsimd
    def _(pool):
        def load(b, par):
            ex = expert_of(pool, keep, b)
            pool.wait_ge(y_taken, b + 1)
            pool.dma_start(w2[:, par].rearrange("p c h f d -> p c h (f d)"),
                           io["wsplit"][bass.ds(ex, 1), :, KC:NPIECE].rearrange("a p c h f -> p (a c) h f"))\
                .then_inc(w2_in[par], 16)
            pool.dma_start(b2[:, par], io["b2"][bass.ds(ex, 1), :].broadcast_to([P, D])).then_inc(w2_in[par], 16)

        pool.wait_ge(w1_in[0], 32)
        with pool.Fori(0, NBLK // 2) as i:
            for par in range(2):
                load(i * 2 + par, par)
        load(NBLK - 1, 0)

    @block.tensor
    def _(pe):
        mm = nc.tensor.matmul
        pe.sem_inc(T_done, 2)
        pe.sem_inc(H_done, 2 * PAIRS)
        pe.sem_inc(Y_done, 2)

        def turn(b, par, half):
            pe.wait_ge(xb_in[par], half * 16 + 16)
            pe.wait_ge(xbt_done, b + 1)
            for a in range(2):
                for kc in range(KC):
                    for s in range(BS):
                        ins = nc.tensor.transpose(Tps[par][:].bitcast(F16)[:, bass.ds(((a * KC + kc) * BS + s) * P, P)],
                                                  xb[:, par, s, bass.ds((a * KC + kc) * P, P)], keep["ident16"][:])
            ins.then_inc(T_done, 1)

        def hidden(b, par, half):
            pe.wait_ge(xbt_done, b + 1 + 2)
            pe.wait_ge(w1_in[par], half * 32 + 32)
            for fc in range(FC):
                if fc % 2 == 0:
                    pe.wait_ge(gelu_done, b * FC + (FC + fc + 2))
                k = 0
                for kc in range(KC):
                    for a, c in ((0, 0), (0, 1), (1, 0)):
                        k += 1
                        ins = mm(Hps[fc // 2][:, fc % 2 * BT:(fc % 2 + 1) * BT], w1[:, par, kc, a, fc * P:(fc + 1) * P],
                                 xbt[:, par, c, kc, :], start=(k == 1), stop=(k == 3 * KC))
                if fc % 2 == 1:
                    ins.then_inc(H_done, 1)

        def down(b, par, half):
            pe.wait_ge(w2_in[par], half * 32 + 32)
            pe.wait_ge(y_taken, b + 1)
            pe.wait_ge(hlo_done, b * 2 + 2 + 4)
            for s in range(BS):
                k = 0
                for fc in range(FC):
                    for a, c in ((0, 0), (0, 1), (1, 0)):
                        k += 1
                        ins = mm(Yps[par][:, s * D:(s + 1) * D], hs[:, par, a, fc, s * P:(s + 1) * P],
                                 w2[:, par, fc // (FC // 2), c, fc % (FC // 2), :],
                                 start=(k == 1), stop=(k == 3 * FC))
            ins.then_inc(Y_done, 1)

        turn(0, 0, 0)
        hidden(0, 0, 0)
        turn(1, 1, 0)
        with pe.Fori(0, NBLK // 2 - 1) as i:
            hidden(i * 2 + 1, 1, i)
            turn(i * 2 + 2, 0, i + 1)
            down(i * 2, 0, i)
            hidden(i * 2 + 2, 0, i + 1)
            turn(i * 2 + 3, 1, i + 1)
            down(i * 2 + 1, 1, i)
        hidden(NBLK - 2, 1, NBLK // 2 - 1)
        turn(NBLK - 1, 0, NBLK // 2)
        down(NBLK - 3, 0, NBLK // 2 - 1)
        hidden(NBLK - 1, 0, NBLK // 2)
        down(NBLK - 2, 1, NBLK // 2 - 1)
        down(NBLK - 1, 0, NBLK // 2)

    @block.scalar
    def _(act):
        act.sem_inc(gelu_done, 2 * FC)
        act.sem_inc(xbt_done, 2)

        def take_x(b, par):
            act.wait_ge(T_done, b + 1 + 2)
            act.wait_ge(H_done, b * PAIRS + PAIRS)
            nc.scalar.activation(xbt[:, par].rearrange("p a c s -> p (a c s)"), Tps[par][:].bitcast(F16),
                                 ACT.Copy).then_inc(xbt_done, 1)

        def gelus(b, par, half):
            act.wait_ge(w1_in[par], half * 32 + 32)
            for fc in range(FC):
                if fc % 2 == 0:
                    act.wait_ge(H_done, b * PAIRS + (fc // 2 + 1 + 2 * PAIRS))
                if fc % (FC // 2) == 0:
                    act.wait_ge(hlo_done, b * 2 + (fc // (FC // 2) + 1 + 2))
                nc.scalar.activation(h32[:, fc, :], Hps[fc // 2][:, fc % 2 * BT:(fc % 2 + 1) * BT],
                                     ACT.Gelu_apprx_tanh, bias=b1[:, par, fc:fc + 1],
                                     scale=1.0 / WSCALE).then_inc(gelu_done, 1)

        take_x(0, 0)
        with act.Fori(0, NBLK // 2) as i:
            gelus(i * 2, 0, i)
            take_x(i * 2 + 1, 1)
            gelus(i * 2 + 1, 1, i)
            take_x(i * 2 + 2, 0)
        gelus(NBLK - 1, 0, NBLK // 2)

    @block.vector
    def _(dve):
        v = nc.vector
        dve.sem_inc(hlo_done, 4)
        dve.sem_inc(y_taken, 2)

        def split_h(b, par):
            dve.wait_ge(Y_done, b + 1)
            for q in range(2):
                fs = slice(q * (FC // 2), (q + 1) * (FC // 2))
                dve.wait_ge(gelu_done, b * FC + ((q + 1) * (FC // 2) + 2 * FC))
                v.tensor_copy(hs[:, par, 0, fs, :], h32[:, fs, :]).then_inc(hhi_done, 1)
                dve.wait_ge(hhi_done, b * 2 + (q + 1))
                v.tensor_tensor(hs[:, par, 1, fs, :], h32[:, fs, :], hs[:, par, 0, fs, :],
                                ALU.subtract).then_inc(hlo_done, 1)

        def take_y(b, par, half):
            dve.wait_ge(Y_done, b + 1 + 2)
            dve.wait_ge(y_out[par], half * 16 + 16)
            v.scalar_tensor_tensor(yo[:, par], Yps[par][:].rearrange("p (s d) -> p s d", d=D), 1.0 / WSCALE,
                                   b2[:, par].unsqueeze(1).broadcast_to([P, BS, D]), ALU.mult,
                                   ALU.add).then_inc(y_taken, 1)

        split_h(0, 0)
        with dve.Fori(0, NBLK // 2 - 1) as i:
            split_h(i * 2 + 1, 1)
            take_y(i * 2, 0, i)
            split_h(i * 2 + 2, 0)
            take_y(i * 2 + 1, 1, i)
        split_h(NBLK - 2, 1)
        take_y(NBLK - 3, 0, NBLK // 2 - 1)
        split_h(NBLK - 1, 0)
        take_y(NBLK - 2, 1, NBLK // 2 - 1)
        take_y(NBLK - 1, 0, NBLK // 2)


def program(nc, io):
    io["xs"] = nc.dram_tensor("xs", [NSLOT, 2 * D], F16).ap()
    io["ys"] = nc.dram_tensor("ys", [NSLOT, D], F32).ap()
    io["wsplit"] = nc.dram_tensor("wsplit", [E, P, NPIECE, 2, PIECE], F16).ap()
    io["x_tok"] = io["x"].rearrange("b (i p) d -> p (b i) d", p=P)
    io["out_tok"] = io["out"].rearrange("b (i p) d -> p (b i) d", p=P)
    with ExitStack() as ctx:
        keep = {}

        def kp(name, shape, dt):
            keep[name] = ctx.enter_context(nc.sbuf_tensor(f"k_{name}", shape, dt))

        kp("WB", [P, 2, KC, N, D], F16)
        kp("WC", [P, 2, KC, N, D], F16)
        kp("xT", [P, NCH, 2, KC, CH], F16)
        kp("Wd", [P, 2, KC, D], F16)
        kp("rel", [P, KC, CH], F32)
        kp("zt", [P, KC, CH], F32)
        kp("dcur", [P, KC, CH], F32)
        kp("yall", [P, NCH, KC, CH], F32)
        kp("A", [P, KC, N], F32)
        kp("rA", [P, KC, N], F32)
        kp("dbias", [P, KC], F32)
        kp("ident", [P, P], F32)
        kp("ident16", [P, P], F16)
        kp("w", [P, 2, NT], F32)
        kp("slot", [P, 2, NT], U32)
        kp("eblk", [P, NBLK], I32)
        keep["scattered"] = ctx.enter_context(nc.semaphore("scattered"))
        keep["w1"] = keep["xT"][:, 0:RCH].rearrange("p a b c d -> p (a b c d)").rearrange(
            "p (r c h f) -> p r c h f", r=2, c=KC, h=2)
        keep["xb"] = keep["yall"][:, RCH].rearrange("p a b -> p (a b)").bitcast(F16).rearrange(
            "p (r s d) -> p r s d", r=2, s=BS)
        keep["b1"] = keep["yall"][:, RCH + 1, 0, 0:2 * FC].rearrange("p (r c) -> p r c", r=2)
        for name in ("w1_in", "xb_in", "y_out"):
            keep[name] = [ctx.enter_context(nc.semaphore(f"{name}{k}")) for k in range(2)]
        keep["zeros_out"] = ctx.enter_context(nc.semaphore("zeros_out"))
        banks = [ctx.enter_context(nc.psum_tensor(f"bank{i}", [P, 512], F32)) for i in range(8)]
        with ExitStack() as rows_ctx:
            keep["x"] = rows_ctx.enter_context(nc.sbuf_tensor("xrows", [P, NT, D], F32))
            keep["rows"] = keep["x"][:].bitcast(F16).rearrange("p t (a d) -> p t a d", a=2)
            with ExitStack() as c1:
                prologue(nc, io, keep, banks, c1)
            with ExitStack() as c1:
                scan_phase(nc, io, keep, banks, c1, 0)
        with ExitStack() as c1:
            expert_phase(nc, io, keep, banks, c1)
        with ExitStack() as c1:
            scan_phase(nc, io, keep, banks, c1, 1)


def kernel(**inputs):
    import numpy as np
    import concourse.bacc as bacc
    from concourse.bass_utils import run_bass_kernel_spmd

    a = {k: np.asarray(v) for k, v in inputs.items()}
    arrays = {
        "x": a["L0_attn_x"],
        "A": a["L0_attn_A"],
        "WdT": a["L0_attn_W_delta"].T,
        "dbias": a["L0_attn_delta_bias"].reshape(KC, P).T,
        "WBT": a["L0_attn_W_B"].reshape(D, N, D).transpose(2, 1, 0).reshape(D, N * D),
        "WCT": a["L0_attn_W_C"].reshape(D, N, D).transpose(2, 1, 0).reshape(D, N * D),
        "W1": a["L0_ffn_W1"],
        "b1": a["L0_ffn_b1"].reshape(E, FC, P).transpose(0, 2, 1),
        "W2": a["L0_ffn_W2"],
        "b2": a["L0_ffn_b2"],
        "Wr": a["L0_ffn_Wr"],
        "br": a["L0_ffn_br"],
    }
    arrays = {k: np.ascontiguousarray(v) for k, v in arrays.items()}
    nc = bacc.Bacc("TRN2", target_bir_lowering=False, num_devices=1)
    io = {k: nc.dram_tensor(f"in_{k}", v.shape, mybir.dt.from_np(v.dtype), kind="ExternalInput").ap()
          for k, v in arrays.items()}
    io["out"] = nc.dram_tensor("out", (B, L, D), F32, kind="ExternalOutput").ap()
    program(nc, io)
    r = run_bass_kernel_spmd(nc, [{f"in_{k}": v for k, v in arrays.items()}], core_ids=[0])
    return r.results[0]["out"]
```
